# Optimizing a Trainium2 kernel written in Bass

```python
import numpy as np
import jax
import jax.numpy as jnp

def _softmax(x, axis=-1):
    return jax.nn.softmax(x, axis=axis)

def _gelu(x):
    return jax.nn.gelu(x, approximate=True)

def _silu(x):
    return jax.nn.silu(x)

def _sigmoid(x):
    return jax.nn.sigmoid(x)

def _layernorm(x, axis=-1, eps=1e-05):
    m = jnp.mean(x, axis=axis, keepdims=True)
    v = jnp.var(x, axis=axis, keepdims=True)
    return (x - m) / jnp.sqrt(v + eps)

def _scatter_add(tgt, idx, src, axis=0):
    return tgt.at[idx].add(src)

def _segment_sum(src, seg, n):
    return jax.ops.segment_sum(src, seg, n)
kernel_name = 'mk_metaformer_d1_conv_nchw256_r2_66d7ad'

def setup_inputs(seed: int=0):
    np.random.seed(seed)
    _w = jnp.asarray

    def _rec_inputs():
        import jax
        import jax.numpy as jnp
        _gk = jax.random.key(seed)
        x = -0.000125 + 0.9999 * jax.random.normal(jax.random.fold_in(_gk, 1), (32, 128, 32, 32), jnp.float32)
        return x
    x = _rec_inputs()

    def _L0_conv_setup():
        import jax, jax.numpy as jnp
        from jax import lax
        import numpy as np
        K = 3
        PAD = 1
        STRIDE = 1
        key = jax.random.key(seed)
        ks = jax.random.split(key, 6)
        b, c, h, w = (32, 128, 32, 32)
        dim = 128
        x = jax.random.normal(ks[0], (b, c, h, w), dtype=jnp.float32)
        w1 = jax.random.normal(ks[1], (dim * K * K, dim), dtype=jnp.float32) * 0.02
        b1 = jax.random.normal(ks[2], (dim * K * K,), dtype=jnp.float32) * 0.02
        w2 = jax.random.normal(ks[3], (dim * K * K, dim), dtype=jnp.float32) * 0.02
        b2 = jax.random.normal(ks[4], (dim * K * K,), dtype=jnp.float32) * 0.02
        bias = jnp.zeros((dim,), dtype=jnp.float32)
        return {'x': x, 'w1': w1, 'b1': b1, 'w2': w2, 'b2': b2, 'bias': bias}
    _L0_conv_all = _L0_conv_setup()
    _L0_conv_in = {k: v for k, v in _L0_conv_all.items() if k in ('w1', 'b1', 'w2', 'b2', 'bias')}
    del _L0_conv_all

    def _L0_ffn_setup():
        import jax, jax.numpy as jnp
        import numpy as np
        TOP_K = 2
        key = jax.random.key(seed)
        ks = jax.random.split(key, 4)
        B, L, D, H, E = (8, 2048, 128, 512, 8)
        s = 0.02
        return {'x': jax.random.normal(ks[0], (B, L, D), jnp.float32), 'Wg': jax.random.normal(ks[1], (D, E), jnp.float32) * s, 'bg': jnp.zeros((E,), jnp.float32), 'W1': jax.random.normal(ks[2], (E, D, H), jnp.float32) * s, 'b1': jnp.zeros((E, H), jnp.float32), 'W2': jax.random.normal(ks[3], (E, H, D), jnp.float32) * s, 'b2': jnp.zeros((E, D), jnp.float32)}
    _L0_ffn_all = _L0_ffn_setup()
    _L0_ffn_in = {k: v for k, v in _L0_ffn_all.items() if k in ('Wg', 'bg', 'W1', 'b1', 'W2', 'b2')}
    del _L0_ffn_all
    return {'x': x, 'L0_conv_w1': _L0_conv_in['w1'], 'L0_conv_b1': _L0_conv_in['b1'], 'L0_conv_w2': _L0_conv_in['w2'], 'L0_conv_b2': _L0_conv_in['b2'], 'L0_conv_bias': _L0_conv_in['bias'], 'L0_ffn_Wg': _L0_ffn_in['Wg'], 'L0_ffn_bg': _L0_ffn_in['bg'], 'L0_ffn_W1': _L0_ffn_in['W1'], 'L0_ffn_b1': _L0_ffn_in['b1'], 'L0_ffn_W2': _L0_ffn_in['W2'], 'L0_ffn_b2': _L0_ffn_in['b2']}

def reference(x, L0_conv_w1, L0_conv_b1, L0_conv_w2, L0_conv_b2, L0_conv_bias, L0_ffn_Wg, L0_ffn_bg, L0_ffn_W1, L0_ffn_b1, L0_ffn_W2, L0_ffn_b2):
    import jax
    import jax.numpy as jnp

    def _L0_conv_ref(x, w1, b1, w2, b2, bias):
        import jax, jax.numpy as jnp
        from jax import lax
        import numpy as np
        K = 3
        PAD = 1
        STRIDE = 1
        b, c, h, w = x.shape
        avg = jnp.mean(x, axis=(2, 3))
        mx = jnp.max(x, axis=(2, 3))
        a = avg @ w1.T + b1
        m = mx @ w2.T + b2
        wt = (m - a).reshape(b * c, 1, K, K)
        wt = jax.nn.softmax(wt, axis=1)
        xr = x.reshape(1, b * c, h, w)
        y = lax.conv_general_dilated(xr, wt, window_strides=(STRIDE, STRIDE), padding=((PAD, PAD), (PAD, PAD)), feature_group_count=b * c, dimension_numbers=('NCHW', 'OIHW', 'NCHW'))
        y = y + jnp.tile(bias, b)[None, :, None, None]
        y = y.reshape(b, c, h, w)
        return y + x

    def _L0_ffn_ref(x, Wg, bg, W1, b1, W2, b2):
        import jax, jax.numpy as jnp
        import numpy as np
        TOP_K = 2
        B, L, D = x.shape
        E = W1.shape[0]
        xf = x.reshape(-1, D)
        gate_logits = xf @ Wg + bg
        top_w, top_i = jax.lax.top_k(gate_logits, TOP_K)
        top_w = jax.nn.softmax(top_w, axis=-1)
        w_dense = jnp.sum(jax.nn.one_hot(top_i, E, dtype=xf.dtype) * top_w[..., None], axis=1)
        out = jnp.zeros_like(xf)
        for e in range(E):
            h = jax.nn.gelu(xf @ W1[e] + b1[e], approximate=False)
            out = out + w_dense[:, e:e + 1] * (h @ W2[e] + b2[e])
        return out.reshape(B, L, D)

    def _gn(v, G=32, eps=1e-05):
        B_, C_, H_, W_ = v.shape
        g = v.reshape(B_, G, C_ // G, H_, W_)
        m = jnp.mean(g, axis=(2, 3, 4), keepdims=True)
        s = jnp.var(g, axis=(2, 3, 4), keepdims=True)
        return ((g - m) / jnp.sqrt(s + eps)).reshape(v.shape)

    def _ln_c(v, eps=1e-06):
        m = jnp.mean(v, axis=1, keepdims=True)
        s = jnp.var(v, axis=1, keepdims=True)
        return (v - m) / jnp.sqrt(s + eps)

    def _ln_t(v, eps=1e-05):
        m = jnp.mean(v, axis=-1, keepdims=True)
        s = jnp.var(v, axis=-1, keepdims=True)
        return (v - m) / jnp.sqrt(s + eps)

    def _to_tokens(v):
        B_, C_, H_, W_ = v.shape
        return v.reshape(B_, C_, H_ * W_).transpose(0, 2, 1)

    def _from_tokens(t, like):
        B_, C_, H_, W_ = like.shape
        return t.transpose(0, 2, 1).reshape(B_, C_, H_, W_)
    x = x + _L0_conv_ref(_ln_c(x), L0_conv_w1, L0_conv_b1, L0_conv_w2, L0_conv_b2, L0_conv_bias)
    t = _to_tokens(x)
    t = t + _L0_ffn_ref(_ln_t(t), L0_ffn_Wg, L0_ffn_bg, L0_ffn_W1, L0_ffn_b1, L0_ffn_W2, L0_ffn_b2)
    x = _from_tokens(t, x)
    return x

_drawn_inputs = setup_inputs


def setup_inputs(seed=0):
    import zlib

    import numpy as np

    out = dict(_drawn_inputs(seed))
    spreads = {'L0_conv_bias': (0.0, 0.33),
     'L0_ffn_bg': (0.0, 0.741),
     'L0_ffn_b1': (0.0, 0.8),
     'L0_ffn_b2': (0.0, 0.467)}
    factors = {'L0_ffn_Wg': 3.31, 'L0_ffn_W1': 6.1, 'L0_ffn_W2': 5.562}
    for name, (base, spread) in spreads.items():
        noise = np.random.default_rng([zlib.crc32(name.encode()), seed]).standard_normal(out[name].shape)
        drawn = base * np.exp(spread * noise) if base else spread * noise
        out[name] = jnp.asarray(drawn.astype(out[name].dtype))
    for name, factor in factors.items():
        out[name] = (out[name] * factor).astype(out[name].dtype)
    return out
```

```python
from contextlib import ExitStack

import concourse.bass as bass
from concourse import mybir

ALU = mybir.AluOpType
ACT = mybir.ActivationFunctionType
AX_X = mybir.AxisListType.X
F32 = mybir.dt.float32
F16 = mybir.dt.float16
BF16 = mybir.dt.bfloat16
I32 = mybir.dt.int32
U32 = mybir.dt.uint32

P = 128
TAPS = 9
LN_C_EPS = 1e-6
LN_T_EPS = 1e-5
MASKED = -1e30
WSCALE = 64.0


class Chain:

    def __init__(self, eng, sem, per_round):
        self.eng, self.sem, self.per_round, self.base, self.n = eng, sem, per_round, 0, 0

    def begin(self, n):
        self.base, self.n = n * self.per_round, 0

    def mark(self, ins):
        self.n += 1
        ins.then_inc(self.sem, 1)

    def wait(self):
        self.eng.wait_ge(self.sem, self.base + self.n)

    def link(self, ins):
        self.mark(ins)
        self.wait()

    def end(self):
        assert self.n == self.per_round, (self.n, self.per_round)


def conv_moe_block(nc, x, conv_w1, conv_b1, conv_w2, conv_b2, conv_bias, Wg, bg, W1, b1, W2, b2, out):
    NIMG, C, HH, WW = x.shape
    PIX = HH * WW
    NBLK = PIX // P
    NTOK = NIMG * PIX
    E, D, H = W1.shape
    HS = H // P
    HALF = 512
    PW, PH = WW + 2, HH + 2
    assert C == P and D == P and NBLK * P == PIX and NIMG % 2 == 0

    NPAIR = E * (E - 1) // 2
    UP_A = 2
    NUP = UP_A * (2 * E - UP_A - 1) // 2
    NREG = max(NUP, NPAIR - NUP)
    CAP = NTOK + 2 * P
    OFF = [a * (2 * E - a - 1) // 2 for a in range(E - 1)]
    NT = NTOK // P + NPAIR
    NT_COLS = -(-NT // P)
    RW = D + 4
    W_LO, W_HI, ID = D, D + 1, D + 2

    rows_dram = nc.dram_tensor("rows_by_pair", [NREG * CAP + P, RW], F32).ap()
    x1_dram = nc.dram_tensor("conv_out", [NIMG, P, PIX], F32).ap()
    y_dram = nc.dram_tensor("expert_out", [NTOK, D], F32).ap()
    tab_dram = nc.dram_tensor("tile_table", [NT_COLS * P, 4], I32).ap()

    x_v = x.rearrange("n c h w -> n c (h w)")
    out_v = out.rearrange("n c h w -> n c (h w)")
    row = lambda v, n: v.rearrange("(a n) -> a n", a=1)

    with ExitStack() as ctx:
        def sb(name, shape, dt=F32):
            return ctx.enter_context(nc.sbuf_tensor(name, shape, dt))

        def psum(name, cols):
            return ctx.enter_context(nc.psum_tensor(name, [P, cols], F32))

        def sem(name):
            return ctx.enter_context(nc.semaphore(name))

        ones = sb("ones", [P, P])
        mean_w = sb("mean_w", [P, P])
        ident = sb("ident", [P, P])
        tri = sb("tri", [P, P])
        tri_b = sb("tri_b", [P, P], BF16)
        ones_b = sb("ones_b", [P, P], BF16)
        eps_c = sb("eps_c", [P, 1])
        eps_t = sb("eps_t", [P, 1])
        desc = sb("desc", [P, E])
        pair_base = sb("pair_base", [P, NPAIR])
        tok_id = sb("tok_id", [P, NBLK])
        tile_no = sb("tile_no", [P, NT_COLS])
        pad_rows = sb("pad_rows", [P, RW])
        bias_sel = sb("bias_sel", [P, P], F16)

        stage = sb("stage", [P, E * H])
        w1h, w1l = sb("w1h", [P, E * H], F16), sb("w1l", [P, E * H], F16)
        w2h, w2l = sb("w2h", [P, E * H], F16), sb("w2l", [P, E * H], F16)
        b1col = sb("b1col", [P, E * HS])
        b1row = sb("b1row", [E * HS, P])
        b2st = sb("b2st", [P, E * D])
        b2row = sb("b2row", [P, E * D], F16)
        b2low = sb("b2low", [P, E * D], F16)
        cw = sb("cw", [P, 2, TAPS * P])
        cwT = sb("cwT", [P, 2, TAPS, P])
        cb = sb("cb", [P, 2, TAPS])
        conv_b = sb("conv_b", [P, 1])
        wg = sb("wg", [P, E])
        wgc = sb("wgc", [P, E])
        bgrow = sb("bgrow", [1, E])
        bgb = sb("bgb", [P, E])

        psA = psum("psA", 1024)
        psV = psum("psV", 1024)
        psT = psum("psT", 1024)
        psG = psum("psG", 512)
        psR = psum("psR", 512)

        s_load = sem("weights_loaded")
        s_stage = sem("stage_loaded")
        s_const = sem("constants_made")
        s_setup_pe = sem("setup_products")
        s_setup_act = sem("setup_act")
        s_setup_dve = sem("setup_dve")
        x_in = [sem(f"x_in{q}") for q in range(2)]
        mean_ready, xc_ready, sq_ready, var_ready, sd_ready = map(
            sem, ("mean_ready", "xc_ready", "sq_ready", "var_ready", "sd_ready"))
        l_ready, max_ready, sum_ready = map(sem, ("l_ready", "max_ready", "sum_ready"))
        tap_ready, z_ready, ez_ready = map(sem, ("tap_ready", "z_ready", "ez_ready"))
        x1_ready = sem("x1_ready")
        x1_out = [sem(f"x1_out{q}") for q in range(2)]
        tok_ready, gate_ready, stat_ready, std_ready, nmr_ready, xn_ready = map(
            sem, ("tok_ready", "gate_ready", "stat_ready", "std_ready", "nmr_ready", "xn_ready"))
        gap_ready, e2_ready, pairs_ready, rank_ready, idx_ready = map(
            sem, ("gap_ready", "e2_ready", "pairs_ready", "rank_ready", "idx_ready"))
        rows_out = [sem(f"rows_out{q}") for q in range(2)]
        ch1, ch2, ch3, chb, chd, cha = map(sem, ("dve_s1", "dve_s2", "dve_s3", "dve_b", "dve_d", "act_a"))
        tab_ready, tab_out, tab_in, padded = map(sem, ("tab_ready", "tab_out", "tab_in", "padded"))
        row_in = [sem(f"row_in{r}") for r in range(4)]
        y_out = [sem(f"y_out{r}") for r in range(4)]
        xT_ready, xh_done, xl_done, h_ready, g_done, hi_done, lo_done, y_ready, yt_done = map(
            sem, ("xT_ready", "xh_done", "xl_done", "h_ready", "g_done", "hi_done", "lo_done", "y_ready",
                  "yt_done"))
        yx_in = [sem(f"yx_in{q}") for q in range(2)]
        yT_ready, o_ready = sem("yT_ready"), sem("o_ready")
        o_out = [sem(f"o_out{q}") for q in range(2)]

        xb = [sb(f"xb{q}", [P, PIX]) for q in range(2)]
        xc = sb("xc", [P, PIX])
        sq = sb("sq", [P, PIX])
        sd = sb("sd", [P, PIX])
        lp = [sb(f"lp{q}", [P, PH, PW]) for q in range(2)]
        junk = sb("junk", [P, PIX])
        pooled = [sb(f"pooled{q}", [P, 2]) for q in range(2)]
        z = sb("z", [P, TAPS])
        zt = sb("zt", [P, TAPS])
        zm = sb("zm", [P, TAPS])
        zd = sb("zd", [P, TAPS])
        ez = sb("ez", [P, TAPS])
        taps = sb("taps", [P, TAPS])
        x1 = [sb(f"x1_{q}", [P, PIX]) for q in range(2)]
        rows = [sb(f"rows{q}", [P, NBLK, RW]) for q in range(2)]
        st = sb("st", [P, NBLK, 6])
        mv = sb("mv", [P, NBLK, 2])
        std = sb("std", [P, NBLK])
        rstd = sb("rstd", [P, NBLK])
        nmr = sb("nmr", [P, NBLK])
        lg, lg2, eq, sc, m1h, m2h, mh = (sb(n, [P, NBLK, E]) for n in ("lg", "lg2", "eq", "sc", "m1h", "m2h", "mh"))
        m1, m2, s1, s2, gap, e2, den, wa, wb, flag, dw, fd, idf = (
            sb(n, [P, NBLK]) for n in ("m1", "m2", "s1", "s2", "gap", "e2", "den", "wa", "wb", "flag", "dw", "fd", "idf"))
        pairs = sb("pairs", [P, NBLK, NPAIR], BF16)
        pos = sb("pos", [P, NBLK, NPAIR])
        base = sb("base", [P, NPAIR])
        idx = [sb(f"idx{q}", [P, NBLK], I32) for q in range(2)]

        cnt, tiles_f, tend, zero28, ge, sel = (sb(n, [P, NPAIR]) for n in ("cnt", "tiles_f", "tend", "zero28", "ge", "sel"))
        cnt_i, tiles_i = sb("cnt_i", [P, NPAIR], I32), sb("tiles_i", [P, NPAIR], I32)
        base_i = sb("base_i", [P, NPAIR], I32)
        tp, tst, trow, ta, tb_, tt1, down_ = (sb(n, [P, NT_COLS]) for n in ("tp", "tst", "trow", "ta", "tb", "tt1", "grows_down"))
        tabt = sb("tabt", [P, NT_COLS, 4], I32)
        tab = sb("tab", [1, NT_COLS * P * 4], I32)

        rt = [sb(f"rt{r}", [P, RW]) for r in range(4)]
        xh = [sb(f"xh{q}", [P, P], F16) for q in range(2)]
        xl = [sb(f"xl{q}", [P, P], F16) for q in range(2)]
        g = [sb(f"g{r}", [P, H]) for r in range(4)]
        gh = [sb(f"gh{r}", [P, H], F16) for r in range(4)]
        gl = [sb(f"gl{r}", [P, H], F16) for r in range(4)]
        yt = [sb(f"yt{r}", [P, D]) for r in range(4)]

        ye = [sb(f"ye{q}", [P, NBLK, D]) for q in range(2)]
        xe = [sb(f"xe{q}", [P, PIX]) for q in range(2)]
        oe = [sb(f"oe{q}", [P, PIX]) for q in range(2)]

        inner = lambda q: lp[q][:, 1:1 + HH, 1:1 + WW]
        img = lambda t: t[:, :].rearrange("p (h w) -> p h w", w=WW)
        spread = lambda t: t[:, :].unsqueeze(2).broadcast_to([P, NBLK, E])
        per_blk = lambda t, n: t[:, :].unsqueeze(1).broadcast_to([P, NBLK, n])

        def hbank(u):
            return (psV[:, 0:512], psV[:, 512:1024], psT[:, 0:512], psT[:, 512:1024])[u % 4]

        def ybank(q):
            return (psG, psR)[q]

        block = ctx.enter_context(nc.Block())

        @block.sync
        def _(sp):
            for free in (*x1_out, *o_out):
                sp.sem_inc(free, 16)
            for dst, src in (
                (cw[:, 0, :], conv_w1.rearrange("(c k) j -> c (k j)", k=TAPS)),
                (cw[:, 1, :], conv_w2.rearrange("(c k) j -> c (k j)", k=TAPS)),
                (cb[:, 0, :], conv_b1.rearrange("(c k) -> c k", k=TAPS)),
                (cb[:, 1, :], conv_b2.rearrange("(c k) -> c k", k=TAPS)),
                (conv_b[:, :], conv_bias.rearrange("(c a) -> c a", a=1)),
                (wg[:, :], Wg), (bgrow[:, :], row(bg, E)),
                (b1row[:, :], b1.rearrange("e (s p) -> (e s) p", p=P)),
            ):
                sp.dma_start(dst, src).then_inc(s_load, 16)
            sp.dma_start(stage[:, :].rearrange("p (e h) -> p e h", e=E), W1.rearrange("e d h -> d e h")).then_inc(s_stage, 16)

            def load(n, q):
                sp.dma_start(xb[q][:, :], x_v[n] if isinstance(n, int) else x_v[bass.ds(n, 1)].rearrange("a c m -> (a c) m")).then_inc(x_in[q], 16)
            load(0, 0)
            load(1, 1)
            sp.wait_ge(s_const, 1)
            b2_flat = b2.rearrange("(a e) d -> a (e d)", a=1)
            sp.dma_start(b2st[0:1, :], b2_flat).then_inc(s_load, 16)
            sp.dma_start(b2st[32:33, :], b2_flat).then_inc(s_load, 16)
            sp.wait_ge(s_setup_dve, 1)
            sp.dma_start(stage[:, :].rearrange("p (e s d) -> p e s d", e=E, s=HS), W2.rearrange("e (s p) d -> p e s d", p=P)).then_inc(s_stage, 16)

            def store(n, q):
                src = x1_dram[n] if isinstance(n, int) else x1_dram[bass.ds(n, 1)].rearrange("a c m -> (a c) m")
                sp.dma_start(src, x1[q][:, :]).then_inc(x1_out[q], 16)
            with sp.Fori(1, NIMG // 2, 1) as t:
                for q in range(2):
                    sp.wait_ge(x1_ready, 2 * t + q - 1)
                    load(2 * t + q, q)
                    store(2 * t + q - 2, q)
            for q in range(2):
                sp.wait_ge(x1_ready, NIMG - 1 + q)
                store(NIMG - 2 + q, q)

            sp.wait_ge(tab_ready, 1)
            for k in range(NPAIR + 1):
                if k < NUP:
                    first = sp.value_load(base_i[0:1, k:k + 1], min_val=k * CAP, max_val=k * CAP + NTOK)
                elif k < NPAIR:
                    top = (k - NUP + 1) * CAP - 1
                    first = sp.value_load(base_i[0:1, k:k + 1], min_val=top - NTOK, max_val=top) - (P - 1)
                else:
                    first = NREG * CAP
                sp.dma_start(rows_dram[bass.ds(first, P), :], pad_rows[:, :]).then_inc(padded, 16)
            sp.wait_ge(tab_ready, 2)
            sp.dma_start(tab_dram.rearrange("(c p) f -> p c f", p=P), tabt[:, :, :]).then_inc(tab_out, 16)
            sp.wait_ge(tab_out, 16)
            sp.dma_start(tab[:, :], tab_dram.rearrange("(a n) f -> a (n f)", a=1)).then_inc(tab_in, 16)
            sp.wait_ge(tab_in, 16)

            sp.wait_ge(padded, 16 * (NPAIR + 1))
            for q in range(2):
                sp.wait_ge(rows_out[q], 16 * NBLK * (NIMG // 2))
            for r in range(4):
                first = sp.value_load(tab[0:1, 4 * r:4 * r + 1], min_val=0, max_val=NREG * CAP)
                sp.dma_start(rt[r][:, :], rows_dram[bass.ds(first, P), :]).then_inc(row_in[r], 16)
            with sp.Fori(1, NT // 4, 1) as t:
                for r in range(4):
                    first = sp.value_load(tab[0:1, bass.ds((4 * t + r) * 4, 1)], min_val=0, max_val=NREG * CAP)
                    sp.wait_ge(y_out[r], 16 * t)
                    sp.dma_start(rt[r][:, :], rows_dram[bass.ds(first, P), :]).then_inc(row_in[r], 16)

            for r in range(4):
                sp.wait_ge(y_out[r], 16 * (NT // 4))
            with sp.Fori(0, NIMG // 2, 1) as t:
                for q in range(2):
                    n = 2 * t + q
                    sp.wait_ge(o_out[q], 16 + 16 * t)
                    sp.dma_start(ye[q][:, :, :], y_dram.rearrange("(n b p) d -> n p b d", b=NBLK, p=P)[bass.ds(n, 1)].rearrange("a p b d -> (a p) b d")).then_inc(yx_in[q], 16)
                    sp.dma_start(xe[q][:, :], x1_dram[bass.ds(n, 1)].rearrange("a c m -> (a c) m")).then_inc(yx_in[q], 16)
            for q in range(2):
                sp.wait_ge(o_out[q], 16 + 16 * (NIMG // 2))
                sp.wait_ge(x1_out[q], 16 + 16 * (NIMG // 2))

        @block.gpsimd
        def _(pool):
            gp = nc.gpsimd
            gp.memset(b2st[:, :], 0.0).then_inc(s_const, 1)
            gp.memset(ones[:, :], 1.0)
            gp.memset(ones_b[:, :], 1.0)
            gp.memset(mean_w[:, :], 1.0 / C)
            gp.memset(eps_c[:, :], LN_C_EPS)
            gp.memset(eps_t[:, :], LN_T_EPS)
            gp.memset(bias_sel[:, :], 0.0)
            gp.memset(zero28[:, :], 0.0)
            for q in range(2):
                gp.memset(lp[q][:, :, :], 0.0)
            gp.memset(pad_rows[:, :], 0.0)
            gp.iota(desc[:, :], [[-1, E]], base=E, channel_multiplier=0, allow_small_or_imprecise_dtypes=True)
            gp.iota(tok_id[:, :], [[P, NBLK]], base=-PIX, channel_multiplier=1, allow_small_or_imprecise_dtypes=True)
            gp.iota(tile_no[:, :], [[P, NT_COLS]], base=0, channel_multiplier=1, allow_small_or_imprecise_dtypes=True)
            gp.iota(pair_base[:, :], [[1, NPAIR]], base=0, channel_multiplier=0,
                    allow_small_or_imprecise_dtypes=True).then_inc(s_const, 1)
            pool.wait_ge(s_const, 2)
            gp.iota(pad_rows[:, ID:ID + 1].bitcast(I32), [[0, 1]], base=NTOK, channel_multiplier=1)
            gp.affine_select(out=ident[:, :], in_=ones[:, :], compare_op=ALU.is_equal, fill=0.0, base=0,
                             pattern=[[-1, P]], channel_multiplier=1)
            gp.affine_select(out=tri[:, :], in_=ones[:, :], compare_op=ALU.is_gt, fill=0.0, base=0,
                             pattern=[[1, P]], channel_multiplier=-1).then_inc(s_const, 1)

            images = pool.alloc_register("images")
            tiles = pool.alloc_register("tiles")
            pool.reg_mov(images, 0)
            pool.reg_mov(tiles, 2)

            def scatter(n, count, q):
                pool.reg_alu(images, images, 1, ALU.add)
                pool.wait_ge(s_const, 3)
                pool.wait_ge(idx_ready, images)
                pool.wait_ge(xn_ready, images)
                for b in range(NBLK):
                    gp.indirect_dma_start(rows_dram, bass.IndirectOffsetOnAxis(ap=idx[q][:, b:b + 1].bitcast(U32), axis=0),
                                          rows[q][:, b, :], None).then_inc(rows_out[q], 16)
            with pool.Fori(0, NIMG // 2, 1) as t:
                for q in range(2):
                    scatter(2 * t + q, t, q)

            with pool.Fori(0, NT // 4, 1) as t:
                for r in range(4):
                    pool.reg_alu(tiles, tiles, 1, ALU.add)
                    pool.wait_ge(s_const, 3)
                    pool.wait_ge(yt_done, tiles)
                    gp.indirect_dma_start(y_dram, bass.IndirectOffsetOnAxis(ap=rt[r][:, ID:ID + 1].bitcast(U32), axis=0),
                                          yt[r][:, :], None, bounds_check=NTOK - 1, oob_is_err=False).then_inc(y_out[r], 16)

        @block.scalar
        def _(act):
            sc_ = nc.scalar
            act.wait_ge(s_stage, 16)
            sc_.activation(w1h[:, :], stage[:, :], ACT.Copy, scale=WSCALE).then_inc(s_setup_act, 1)
            act.wait_ge(s_load, 16 * 10)
            sc_.activation(b2row[:, :], b2st[:, :], ACT.Copy, scale=WSCALE).then_inc(s_setup_act, 1)
            for n in range(5):
                act.wait_ge(s_setup_pe, n + 1)
                k = min(4, 2 * TAPS - 4 * n)
                sc_.activation(cwT[:, :, :, :].rearrange("p a k c -> p (a k) c")[:, 4 * n:4 * n + k, :],
                               (psA if n % 2 == 0 else psV)[:, 0:k * P].rearrange("p (k c) -> p k c", c=P), ACT.Copy).then_inc(s_setup_act, 1)
            act.wait_ge(s_setup_pe, 6)
            sc_.activation(b1col[:, :], psG[:, 0:E * HS], ACT.Copy).then_inc(s_setup_act, 1)
            sc_.activation(bgb[:, :], psG[:, 64:64 + E], ACT.Copy).then_inc(s_setup_act, 1)
            act.wait_ge(s_stage, 32)
            sc_.activation(w2h[:, :], stage[:, :], ACT.Copy, scale=WSCALE).then_inc(s_setup_act, 1)
            act.wait_ge(s_const, 3)

            def step(i1, i2, i3, q):
                if i1 is not None:
                    act.wait_ge(xc_ready, i1 + 1)
                    sc_.activation(sq[:, :], xc[:, :], ACT.Square).then_inc(sq_ready, 1)
                if i2 is not None:
                    act.wait_ge(z_ready, i2 + 1)
                    sc_.activation(ez[:, :], zd[:, :], ACT.Exp).then_inc(ez_ready, 1)
                if i1 is not None:
                    act.wait_ge(var_ready, i1 + 1)
                    sc_.activation(sd[:, :], psV[:, :], ACT.Sqrt, bias=eps_c[:, :]).then_inc(sd_ready, 1)
                if i3 is not None:
                    act.wait_ge(stat_ready, i3 + 1)
                    sc_.activation(std[:, :], mv[:, :, 1], ACT.Sqrt, bias=eps_t[:, :]).then_inc(std_ready, 1)
                if i1 is not None:
                    act.wait_ge(l_ready, i1 + 1)
                    sc_.activation(img(junk), inner(q), ACT.Copy, accum_out=pooled[q][:, 0:1]).then_inc(sum_ready, 1)
                if i3 is not None:
                    act.wait_ge(nmr_ready, i3 + 1)
                    yield_rows(i3, q)
                    for b in range(NBLK):
                        last = sc_.activation(rows[q][:, b, 0:D], psT[:, b * P:(b + 1) * P], ACT.Identity,
                                              bias=nmr[:, b:b + 1], scale=rstd[:, b:b + 1])
                    last.then_inc(xn_ready, 1)
                    act.wait_ge(gap_ready, i3 + 1)
                    sc_.activation(e2[:, :], gap[:, :], ACT.Exp).then_inc(e2_ready, 1)

            def yield_rows(i3, q):
                if isinstance(i3, int):
                    if i3 >= 2:
                        act.wait_ge(rows_out[q], 16 * NBLK * (i3 // 2))
                else:
                    act.wait_ge(rows_out[q], 16 * NBLK * turn[0])

            turn = [None]
            step(0, None, None, 0)
            step(1, 0, None, 1)
            step(2, 1, 0, 0)
            step(3, 2, 1, 1)
            with act.Fori(2, NIMG // 2, 1) as t:
                for q in range(2):
                    turn[0] = t - 1
                    step(2 * t + q, 2 * t + q - 1, 2 * t + q - 2, q)
            step(None, NIMG - 1, NIMG - 2, 0)
            step(None, None, NIMG - 1, 1)

            act.wait_ge(tab_in, 16)

            def high(j, q):
                act.wait_ge(xT_ready, j + 1)
                sc_.activation(xh[q][:, :], psA[:, 512 * q:512 * q + P], ACT.Copy).then_inc(xh_done, 1)

            def gelu(j, side, r):
                e = act.value_load(tab[0:1, bass.ds(4 * j + 1 + side, 1)] if not isinstance(j, int) else tab[0:1, 4 * j + 1 + side:4 * j + 2 + side], min_val=0, max_val=E - 1)
                act.wait_ge(h_ready, 2 * j + side + 1)
                bank = hbank(2 * r + side)
                for s in range(HS):
                    last = sc_.activation(g[(2 * r + side) % 4][:, s * P:(s + 1) * P], bank[:, s * P:(s + 1) * P], ACT.Gelu,
                                          bias=b1col[:, bass.ds(e * HS + s, 1)], scale=1.0 / WSCALE)
                last.then_inc(g_done, 1)

            high(0, 0)
            high(1, 1)
            gelu(0, 0, 0)
            gelu(0, 1, 0)

            def dstep(j, r):
                if not isinstance(j, int) or j + 2 < NT:
                    high(j + 2, r % 2)
                if not isinstance(j, int) or j + 1 < NT:
                    gelu(j + 1, 0, (r + 1) % 4)
                    gelu(j + 1, 1, (r + 1) % 4)
            with act.Fori(0, NT // 4 - 1, 1) as t:
                for r in range(4):
                    dstep(4 * t + r, r)
            for r in range(4):
                dstep(NT - 4 + r, r)

            with act.Fori(0, NIMG // 2, 1) as t:
                for q in range(2):
                    act.wait_ge(o_ready, 2 * t + q + 3)
                    act.dma_start(out_v[bass.ds(2 * t + q, 1)].rearrange("a c m -> (a c) m"), oe[q][:, :]).then_inc(o_out[q], 16)

        @block.tensor
        def _(pe):
            te = nc.tensor
            pe.wait_ge(s_const, 3)
            pe.wait_ge(s_load, 16 * 10)
            for n in range(5):
                k = min(4, 2 * TAPS - 4 * n)
                if n >= 2:
                    pe.wait_ge(s_setup_act, 2 + n - 1)
                for m in range(k):
                    a, tap = divmod(4 * n + m, TAPS)
                    last = te.transpose((psA if n % 2 == 0 else psV)[:, m * P:(m + 1) * P], cw[:, a, tap * P:(tap + 1) * P], ident[:, :])
                last.then_inc(s_setup_pe, 1)
            te.transpose(psG[:, 0:E * HS], b1row[:, :], ident[0:E * HS, 0:E * HS])
            te.matmul(psG[:, 64:64 + E], ones[0:1, :], bgrow[:, :], start=True, stop=True)
            te.matmul(psG[:, 128:128 + E], mean_w[:, :], wg[:, :], start=True, stop=True).then_inc(s_setup_pe, 1)
            pe.wait_ge(s_setup_act, 9)
            pe.wait_ge(s_setup_dve, 3)

            def step(i1, i2, i3, q):
                if i1 is not None:
                    wait_x(i1, q)
                    if not isinstance(i1, int) or i1 >= 1:
                        pe.wait_ge(xc_ready, i1)
                    for h in range(2):
                        last = te.matmul(psA[:, h * HALF:(h + 1) * HALF], mean_w[:, :], xb[q][:, h * HALF:(h + 1) * HALF], start=True, stop=True)
                    last.then_inc(mean_ready, 1)
                if i2 is not None:
                    pe.wait_ge(sum_ready, i2 + 1)
                    pe.wait_ge(max_ready, i2 + 1)
                    if i1 is not None:
                        pe.wait_ge(xc_ready, i1 + 1)
                    else:
                        pe.wait_ge(pairs_ready, i2 - 1)
                    for a in range(2):
                        for k in range(TAPS):
                            last = te.matmul(psG[:, 256 + a * 16 + k:257 + a * 16 + k], cwT[:, a, k, :], pooled[1 - q][:, a:a + 1], start=True, stop=True)
                    last.then_inc(tap_ready, 1)
                if i3 is not None:
                    pe.wait_ge(x1_ready, i3 + 1)
                    if i2 is not None:
                        pe.wait_ge(z_ready, i2 + 1)
                    if not isinstance(i3, int) or i3 >= 1:
                        pe.wait_ge(xn_ready, i3)
                        pe.wait_ge(pairs_ready, i3)
                    for b in range(NBLK):
                        te.transpose(psT[:, b * P:(b + 1) * P], x1[q][:, b * P:(b + 1) * P], ident[:, :])
                        last = te.matmul(psG[:, b * E:(b + 1) * E], x1[q][:, b * P:(b + 1) * P], wgc[:, :], start=True, stop=True)
                    last.then_inc(tok_ready, 1)
                if i1 is not None:
                    pe.wait_ge(sq_ready, i1 + 1)
                    if not isinstance(i1, int) or i1 >= 1:
                        pe.wait_ge(sd_ready, i1)
                    for h in range(2):
                        last = te.matmul(psV[:, h * HALF:(h + 1) * HALF], mean_w[:, :], sq[:, h * HALF:(h + 1) * HALF], start=True, stop=True)
                    last.then_inc(var_ready, 1)
                if i3 is not None:
                    pe.wait_ge(pairs_ready, i3 + 1)
                    if not isinstance(i3, int) or i3 >= 1:
                        pe.wait_ge(idx_ready, i3)
                    n = NPAIR
                    te.matmul(psR[:, 0:NBLK * n], tri_b[:, :], pairs[:, :, :].rearrange("p b k -> p (b k)"), start=True, stop=False)
                    for b in range(NBLK - 1):
                        left = NBLK - 1 - b
                        te.matmul(psR[:, (b + 1) * n:NBLK * n].rearrange("p (b k) -> p b k", k=n), ones_b[:, :],
                                  pairs[:, b:b + 1, :].broadcast_to([P, left, n]), start=False, stop=(b == NBLK - 2))
                    for b in range(NBLK):
                        last = te.matmul(psR[:, NBLK * n:(NBLK + 1) * n], ones_b[:, :], pairs[:, b, :], start=(b == 0), stop=(b == NBLK - 1))
                    last.then_inc(rank_ready, 1)

            def wait_x(i1, q):
                pe.wait_ge(x_in[q], 16 * (i1 // 2 + 1) if isinstance(i1, int) else 16 * (turn[0] + 1))

            turn = [None]
            step(0, None, None, 0)
            step(1, 0, None, 1)
            with pe.Fori(1, NIMG // 2, 1) as t:
                for q in range(2):
                    turn[0] = t
                    step(2 * t + q, 2 * t + q - 1, 2 * t + q - 2, q)
            step(None, NIMG - 1, NIMG - 2, 0)
            step(None, None, NIMG - 1, 1)

            pe.wait_ge(tab_in, 16)
            pe.wait_ge(idx_ready, NIMG)

            def turn_rows(j, r, t):
                pe.wait_ge(row_in[r], 16 * (t + 1))
                if not isinstance(j, int) or j >= 2:
                    pe.wait_ge(xl_done, j - 1)
                    pe.wait_ge(xh_done, j - 1)
                te.transpose(psA[:, 512 * (r % 2):512 * (r % 2) + P], rt[r][:, 0:D], ident[:, :]).then_inc(xT_ready, 1)

            def expert(j, side):
                at = 4 * j + 1 + side
                return pe.value_load(tab[0:1, at:at + 1] if isinstance(j, int) else tab[0:1, bass.ds(at, 1)], min_val=0, max_val=E - 1)

            def up(j, side, r):
                e = expert(j, side)
                pe.wait_ge(xh_done, j + 1)
                pe.wait_ge(xl_done, j + 1)
                bank = hbank(2 * r + side)
                q = r % 2
                for s in range(HS):
                    col = bass.ds(e * H + s * P, P)
                    o = bank[:, s * P:(s + 1) * P]
                    te.matmul(o, w1h[:, col], xh[q][:, :], start=True, stop=False)
                    te.matmul(o, w1h[:, col], xl[q][:, :], start=False, stop=False)
                    last = te.matmul(o, w1l[:, col], xh[q][:, :], start=False, stop=True)
                last.then_inc(h_ready, 1)

            def down(j, side, r):
                e = expert(j, side)
                u = (2 * r + side) % 4
                pe.wait_ge(hi_done, 2 * j + side + 1)
                pe.wait_ge(lo_done, 2 * j + side + 1)
                if side == 0:
                    pe.wait_ge(yt_done, j + 1)
                o = ybank(r % 2)[:, side * P:(side + 1) * P]
                te.matmul(o, bias_sel[:, :], b2row[:, bass.ds(e * D, D)], start=True, stop=False)
                for s in range(HS):
                    col = bass.ds(e * H + s * P, P)
                    te.matmul(o, gh[u][:, s * P:(s + 1) * P], w2h[:, col], start=False, stop=False)
                    te.matmul(o, gh[u][:, s * P:(s + 1) * P], w2l[:, col], start=False, stop=False)
                    last = te.matmul(o, gl[u][:, s * P:(s + 1) * P], w2h[:, col], start=False, stop=(s == HS - 1))
                last.then_inc(y_ready, 1)

            turn_rows(0, 0, 0)
            turn_rows(1, 1, 0)
            up(0, 0, 0)
            up(0, 1, 0)

            def dstep(j, r, t):
                more = not isinstance(j, int)
                if more or j + 1 < NT:
                    up(j + 1, 0, (r + 1) % 4)
                if more or j + 2 < NT:
                    turn_rows(j + 2, (r + 2) % 4, t + (r + 2) // 4)
                down(j, 0, r)
                if more or j + 1 < NT:
                    up(j + 1, 1, (r + 1) % 4)
                down(j, 1, r)
            with pe.Fori(0, NT // 4 - 1, 1) as t:
                for r in range(4):
                    dstep(4 * t + r, r, t)
            for r in range(4):
                dstep(NT - 4 + r, r, NT // 4 - 1)

            with pe.Fori(0, NIMG // 2, 1) as t:
                for q in range(2):
                    pe.wait_ge(yx_in[q], 32 * (t + 1))
                    pe.wait_ge(o_ready, 2 * t + q + 1)
                    for b in range(NBLK):
                        last = te.transpose((psA if q == 0 else psV)[:, b * P:(b + 1) * P], ye[q][:, b, :], ident[:, :])
                    last.then_inc(yT_ready, 1)

        @block.vector
        def _(dve):
            v = nc.vector
            dve.wait_ge(s_setup_act, 1)
            v.scalar_tensor_tensor(out=w1l[:, :], in0=stage[:, :], scalar=WSCALE, in1=w1h[:, :], op0=ALU.mult, op1=ALU.subtract).then_inc(s_setup_dve, 1)
            dve.wait_ge(s_const, 3)
            v.memset(bias_sel[0:1, :], 1.0)
            v.memset(bias_sel[32:33, :], 1.0)
            v.tensor_copy(tri_b[:, :], tri[:, :])
            v.tensor_scalar(pair_base[:, 0:NUP], pair_base[:, 0:NUP], float(CAP), None, ALU.mult)
            v.tensor_scalar(pair_base[:, NUP:NPAIR], pair_base[:, NUP:NPAIR], float(CAP), float(CAP * (1 - NUP) - 1), ALU.mult, ALU.add).then_inc(s_setup_dve, 1)
            dve.wait_ge(s_setup_dve, 2)
            v.tensor_copy(base[:, :], pair_base[:, :])
            dve.wait_ge(s_setup_act, 2)
            v.scalar_tensor_tensor(out=b2low[:, :], in0=b2st[:, :], scalar=WSCALE, in1=b2row[:, :], op0=ALU.mult, op1=ALU.subtract)
            dve.wait_ge(s_setup_act, 9)
            v.tensor_tensor(wgc[:, :], wg[:, :], psG[:, 128:128 + E], ALU.subtract).then_inc(s_setup_dve, 1)
            dve.wait_ge(s_setup_dve, 3)
            v.tensor_copy(b2row[32:33, :], b2low[32:33, :]).then_inc(s_setup_dve, 1)
            dve.wait_ge(s_setup_act, 10)
            v.scalar_tensor_tensor(out=w2l[:, :], in0=stage[:, :], scalar=WSCALE, in1=w2h[:, :], op0=ALU.mult, op1=ALU.subtract).then_inc(s_setup_dve, 1)

            after_stats = dve.alloc_register("after_stats")
            c1 = Chain(dve, ch1, 1)
            c2 = Chain(dve, ch2, 15)
            c3 = Chain(dve, ch3, 32)

            def step(i1, i2, i3, q):
                if i1 is not None:
                    dve.wait_ge(mean_ready, i1 + 1)
                    dve.wait_ge(x_in[q], 16 * (turn[0] + 1))
                    if not isinstance(i1, int) or i1 >= 1:
                        dve.wait_ge(l_ready, i1)
                    v.tensor_tensor(xc[:, :], xb[q][:, :], psA[:, :], ALU.subtract).then_inc(xc_ready, 1)
                if i2 is not None:
                    c2.begin(i2)
                    dve.wait_ge(tap_ready, i2 + 1)
                    v.scalar_tensor_tensor(out=zt[:, :], in0=psG[:, 256:256 + TAPS], scalar=1.0 / PIX, in1=cb[:, 0, :], op0=ALU.mult, op1=ALU.add)
                    c2.link(v.tensor_tensor(zm[:, :], psG[:, 272:272 + TAPS], cb[:, 1, :], ALU.add))
                    c2.link(v.tensor_tensor(z[:, :], zm[:, :], zt[:, :], ALU.subtract))
                    c2.link(v.tensor_reduce(zt[:, :], z[:, :].unsqueeze(2), AX_X, ALU.max))
                    v.tensor_tensor(zd[:, :], z[:, :], zt[:, :], ALU.subtract).then_inc(z_ready, 1)
                if i3 is not None:
                    c3.begin(i3)
                    dve.wait_ge(tok_ready, i3 + 1)
                    for b in range(NBLK):
                        last = v.bn_stats(st[:, b, :], psT[:, b * P:(b + 1) * P])
                    c3.mark(last)
                    dve.reg_mov(after_stats, c3.base + c3.n)
                    dve.wait_ge(s_const, 3)
                    dve.wait_ge(ch3, after_stats)
                    for b in range(NBLK):
                        last = v.bn_aggr(mv[:, b, :], st[:, b, :])
                    last.then_inc(stat_ready, 1)
                if i1 is not None:
                    dve.wait_ge(sd_ready, i1 + 1)
                    c1.begin(i1)
                    c1.link(v.reciprocal(sd[:, :], sd[:, :]))
                    v.tensor_tensor(inner(q), img(xc), img(sd), ALU.mult).then_inc(l_ready, 1)
                    dve.wait_ge(l_ready, i1 + 1)
                    v.tensor_reduce(pooled[q][:, 1:2], inner(q), mybir.AxisListType.XY, ALU.max).then_inc(max_ready, 1)
                if i3 is not None:
                    dve.wait_ge(std_ready, i3 + 1)
                    c3.link(v.reciprocal(rstd[:, :], std[:, :]))
                    v.scalar_tensor_tensor(out=nmr[:, :], in0=mv[:, :, 0], scalar=-1.0, in1=rstd[:, :], op0=ALU.mult, op1=ALU.mult).then_inc(nmr_ready, 1)
                if i2 is not None:
                    dve.wait_ge(ez_ready, i2 + 1)
                    c2.link(v.tensor_reduce(zm[:, :], ez[:, :].unsqueeze(2), AX_X, ALU.add))
                    c2.link(v.reciprocal(zt[:, :], zm[:, :]))
                    c2.link(v.tensor_tensor(taps[:, :], ez[:, :], zt[:, :], ALU.mult))
                    wait_x1(i2)
                    p = 1 - q
                    c2.link(v.scalar_tensor_tensor(out=img(x1[p]), in0=inner(p), scalar=conv_b[:, :], in1=img(xb[p]), op0=ALU.add, op1=ALU.add))
                    for k in range(TAPS):
                        dy, dx = divmod(k, 3)
                        ins = v.scalar_tensor_tensor(out=img(x1[p]), in0=lp[p][:, dy:dy + HH, dx:dx + WW], scalar=taps[:, k:k + 1],
                                                     in1=img(x1[p]), op0=ALU.mult, op1=ALU.add)
                        if k < TAPS - 1:
                            c2.link(ins)
                        else:
                            ins.then_inc(x1_ready, 1)
                    c2.end()
                if i3 is not None:
                    route(i3, q)

            def wait_x1(i2):
                if isinstance(i2, int):
                    if i2 >= 2:
                        dve.wait_ge(x1_out[i2 % 2], 16 + 16 * (i2 // 2))
                else:
                    dve.wait_ge(x1_out[par[0]], 16 + 16 * par[1])

            def route(i3, q):
                link = c3.link
                link(v.tensor_tensor(lg[:, :, :], psG[:, 0:NBLK * E].rearrange("p (b e) -> p b e", e=E), spread(rstd), ALU.mult))
                link(v.tensor_tensor(lg[:, :, :], lg[:, :, :], per_blk(bgb, E), ALU.add))
                for n, (src, mx, s, mask) in enumerate(((lg, m1, s1, m1h), (lg2, m2, s2, m2h))):
                    if n == 1:
                        link(v.scalar_tensor_tensor(out=lg2[:, :, :], in0=m1h[:, :, :], scalar=MASKED, in1=lg[:, :, :], op0=ALU.mult, op1=ALU.add))
                    link(v.tensor_reduce(mx[:, :], src[:, :, :], AX_X, ALU.max))
                    link(v.tensor_tensor(eq[:, :, :], src[:, :, :], spread(mx), ALU.is_equal))
                    link(v.tensor_tensor(sc[:, :, :], eq[:, :, :], per_blk(desc, E), ALU.mult))
                    link(v.tensor_reduce(s[:, :], sc[:, :, :], AX_X, ALU.max))
                    link(v.tensor_tensor(mask[:, :, :], sc[:, :, :], spread(s), ALU.is_equal))
                v.tensor_tensor(gap[:, :], m2[:, :], m1[:, :], ALU.subtract).then_inc(gap_ready, 1)
                link(v.tensor_tensor(mh[:, :, :], m1h[:, :, :], m2h[:, :, :], ALU.add))
                for a in range(E - 1):
                    n = E - 1 - a
                    last = v.scalar_tensor_tensor(out=pairs[:, :, OFF[a]:OFF[a] + n], in0=mh[:, :, a + 1:E], scalar=1.0 if a < UP_A else -1.0,
                                                  in1=mh[:, :, a:a + 1].broadcast_to([P, NBLK, n]), op0=ALU.mult, op1=ALU.mult)
                last.then_inc(pairs_ready, 1)
                dve.wait_ge(e2_ready, i3 + 1)
                link(v.tensor_scalar(den[:, :], e2[:, :], WSCALE, WSCALE, ALU.mult, ALU.add))
                link(v.reciprocal(wa[:, :], den[:, :]))
                link(v.tensor_tensor(wb[:, :], e2[:, :], wa[:, :], ALU.mult))
                link(v.tensor_tensor(flag[:, :], s1[:, :], s2[:, :], ALU.is_gt))
                link(v.tensor_tensor(dw[:, :], wa[:, :], wb[:, :], ALU.subtract))
                link(v.tensor_tensor(fd[:, :], flag[:, :], dw[:, :], ALU.mult))
                dve.wait_ge(xn_ready, i3 + 1)
                link(v.tensor_tensor(rows[q][:, :, W_LO], wb[:, :], fd[:, :], ALU.add))
                link(v.tensor_tensor(rows[q][:, :, W_HI], wa[:, :], fd[:, :], ALU.subtract))
                link(v.tensor_scalar(tok_id[:, :], tok_id[:, :], float(PIX), None, ALU.add))
                link(v.tensor_copy(rows[q][:, :, ID].bitcast(I32), tok_id[:, :]))
                link(v.memset(rows[q][:, :, ID + 1], 0.0))
                dve.wait_ge(rank_ready, i3 + 1)
                dve.wait_ge(pairs_ready, i3 + 1)
                link(v.tensor_tensor(pos[:, :, :], psR[:, 0:NBLK * NPAIR].rearrange("p (b k) -> p b k", k=NPAIR), per_blk(base, NPAIR), ALU.add))
                link(v.tensor_tensor(pos[:, :, :], pos[:, :, :], pairs[:, :, :], ALU.mult))
                link(v.tensor_reduce(idf[:, :], pos[:, :, :], AX_X, ALU.add))
                link(v.scalar_tensor_tensor(out=idf[:, :], in0=idf[:, :], scalar=-1.0, in1=idf[:, :], op0=ALU.mult, op1=ALU.max))
                link(v.tensor_tensor(base[:, :], base[:, :], psR[:, NBLK * NPAIR:(NBLK + 1) * NPAIR], ALU.add))
                v.tensor_copy(idx[q][:, :], idf[:, :]).then_inc(idx_ready, 1)
                c3.end()

            turn, par = [0], [0, 0]
            step(0, None, None, 0)
            step(1, 0, None, 1)
            with dve.Fori(1, NIMG // 2, 1) as t:
                for q in range(2):
                    turn[0] = t
                    par[:] = [1 - q, t - 1 if q == 0 else t]
                    step(2 * t + q, 2 * t + q - 1, 2 * t + q - 2, q)
            step(None, NIMG - 1, NIMG - 2, 0)
            step(None, None, NIMG - 1, 1)

            cb_ = Chain(dve, chb, 0)
            link = cb_.link
            dve.wait_ge(idx_ready, NIMG)
            v.tensor_copy(base_i[:, :], base[:, :]).then_inc(tab_ready, 1)
            link(v.tensor_tensor(cnt[:, :], base[:, :], pair_base[:, :], ALU.subtract))
            link(v.scalar_tensor_tensor(out=cnt[:, :], in0=cnt[:, :], scalar=-1.0, in1=cnt[:, :], op0=ALU.mult, op1=ALU.max))
            link(v.tensor_scalar(cnt[:, :], cnt[:, :], float(P - 1), None, ALU.add))
            link(v.tensor_copy(cnt_i[:, :], cnt[:, :]))
            link(v.tensor_scalar(tiles_i[:, :], cnt_i[:, :], P.bit_length() - 1, None, ALU.arith_shift_right))
            link(v.tensor_copy(tiles_f[:, :], tiles_i[:, :]))
            link(v.tensor_tensor_scan(tend[:, :], tiles_f[:, :], zero28[:, :], 0.0, ALU.add, ALU.add))
            for c in range(NT_COLS):
                link(v.tensor_scalar(ge[:, :], tend[:, :], tile_no[:, c:c + 1], None, ALU.is_le))
                link(v.tensor_reduce(tp[:, c:c + 1], ge[:, :], AX_X, ALU.add))
                link(v.tensor_tensor(sel[:, :], ge[:, :], tend[:, :], ALU.mult))
                link(v.tensor_reduce(tst[:, c:c + 1], sel[:, :], AX_X, ALU.max))
            link(v.tensor_scalar(trow[:, :], tp[:, :], float(CAP), None, ALU.mult))
            link(v.tensor_tensor(tt1[:, :], tile_no[:, :], tst[:, :], ALU.subtract))
            link(v.scalar_tensor_tensor(out=trow[:, :], in0=tt1[:, :], scalar=float(P), in1=trow[:, :], op0=ALU.mult, op1=ALU.add))
            link(v.tensor_scalar(down_[:, :], tp[:, :], float(NUP), None, ALU.is_ge))
            link(v.tensor_tensor(tt1[:, :], tt1[:, :], down_[:, :], ALU.mult))
            link(v.scalar_tensor_tensor(out=trow[:, :], in0=tt1[:, :], scalar=float(-2 * P), in1=trow[:, :], op0=ALU.mult, op1=ALU.add))
            link(v.scalar_tensor_tensor(out=trow[:, :], in0=down_[:, :], scalar=float(CAP - P - NUP * CAP), in1=trow[:, :], op0=ALU.mult, op1=ALU.add))
            link(v.tensor_scalar(trow[:, :], trow[:, :], float(NREG * CAP), None, ALU.min))
            link(v.memset(ta[:, :], 0.0))
            link(v.tensor_scalar(tb_[:, :], tp[:, :], 1.0, None, ALU.add))
            for s in range(1, E - 1):
                link(v.tensor_scalar(tt1[:, :], tp[:, :], float(OFF[s]), None, ALU.is_ge))
                link(v.tensor_tensor(ta[:, :], ta[:, :], tt1[:, :], ALU.add))
                link(v.scalar_tensor_tensor(out=tb_[:, :], in0=tt1[:, :], scalar=float(1 - OFF[s] + OFF[s - 1]), in1=tb_[:, :],
                                            op0=ALU.mult, op1=ALU.add))
            link(v.tensor_scalar(tb_[:, :], tb_[:, :], float(E - 1), None, ALU.min))
            for f, src in enumerate((trow, ta, tb_)):
                link(v.tensor_copy(tabt[:, :, f], src[:, :]))
            v.memset(tabt[:, :, 3], 0).then_inc(tab_ready, 1)

            cd = Chain(dve, chd, 1)
            dve.sem_inc(yt_done, 2)

            def low(j, q):
                dve.wait_ge(xh_done, j + 1)
                v.tensor_tensor(xl[q][:, :], psA[:, 512 * q:512 * q + P], xh[q][:, :], ALU.subtract).then_inc(xl_done, 1)

            def split(j, side, r):
                u = (2 * r + side) % 4
                dve.wait_ge(g_done, 2 * j + side + 1)
                v.tensor_copy(gh[u][:, :], g[u][:, :]).then_inc(hi_done, 1)
                dve.wait_ge(hi_done, 2 * j + side + 1)
                v.tensor_tensor(gl[u][:, :], g[u][:, :], gh[u][:, :], ALU.subtract).then_inc(lo_done, 1)

            def combine(j, r):
                cd.begin(j)
                dve.wait_ge(y_ready, 2 * j + 2)
                bank = ybank(r % 2)
                cd.link(v.tensor_scalar(yt[r][:, :], bank[:, 0:D], rt[r][:, W_LO:W_LO + 1], None, ALU.mult))
                v.scalar_tensor_tensor(out=yt[r][:, :], in0=bank[:, D:2 * D], scalar=rt[r][:, W_HI:W_HI + 1], in1=yt[r][:, :],
                                       op0=ALU.mult, op1=ALU.add).then_inc(yt_done, 1)

            low(0, 0)
            low(1, 1)
            split(0, 0, 0)
            split(0, 1, 0)

            def dstep(j, r):
                more = not isinstance(j, int)
                if more or j + 2 < NT:
                    low(j + 2, r % 2)
                if more or j + 1 < NT:
                    split(j + 1, 0, (r + 1) % 4)
                    split(j + 1, 1, (r + 1) % 4)
                combine(j, r)
            with dve.Fori(0, NT // 4 - 1, 1) as t:
                for r in range(4):
                    dstep(4 * t + r, r)
            for r in range(4):
                dstep(NT - 4 + r, r)

            dve.sem_inc(o_ready, 2)
            with dve.Fori(0, NIMG // 2, 1) as t:
                for q in range(2):
                    dve.wait_ge(yT_ready, 2 * t + q + 1)
                    dve.wait_ge(yx_in[q], 32 * (t + 1))
                    dve.wait_ge(o_out[q], 16 + 16 * t)
                    v.tensor_tensor(oe[q][:, :], xe[q][:, :], (psA if q == 0 else psV)[:, :], ALU.add).then_inc(o_ready, 1)


_INS = ['x', 'L0_conv_w1', 'L0_conv_b1', 'L0_conv_w2', 'L0_conv_b2', 'L0_conv_bias', 'L0_ffn_Wg', 'L0_ffn_bg',
        'L0_ffn_W1', 'L0_ffn_b1', 'L0_ffn_W2', 'L0_ffn_b2']
_OUTS = [((32, 128, 32, 32), 'float32')]


def kernel(**inputs):
    import numpy as _np
    import concourse.bacc as _bacc
    from concourse import mybir as _mybir
    from concourse.bass_utils import run_bass_kernel_spmd as _run

    nc = _bacc.Bacc("TRN2", target_bir_lowering=False, num_devices=1)
    arrays, args = {}, []
    for name in _INS:
        a = _np.ascontiguousarray(inputs[name])
        arrays[f"in_{name}_dram"] = a
        args.append(nc.dram_tensor(f"in_{name}_dram", a.shape, _mybir.dt.from_np(a.dtype), kind="ExternalInput").ap())
    for i, (shape, dtype) in enumerate(_OUTS):
        dt = _mybir.dt.from_np(_np.dtype(dtype))
        args.append(nc.dram_tensor(f"out_{i}_dram", shape, dt, kind="ExternalOutput").ap())
    conv_moe_block(nc, *args)
    r = _run(nc, [arrays], core_ids=[0])
    got = tuple(r.results[0][f"out_{i}_dram"] for i in range(len(_OUTS)))
    return got[0]
```

```python
from contextlib import ExitStack

import concourse.bass as bass
from concourse import mybir

ALU = mybir.AluOpType
ACT = mybir.ActivationFunctionType
AX_X = mybir.AxisListType.X
F32 = mybir.dt.float32
F16 = mybir.dt.float16
BF16 = mybir.dt.bfloat16
I32 = mybir.dt.int32
U32 = mybir.dt.uint32

P = 128
TAPS = 9
LN_C_EPS = 1e-6
LN_T_EPS = 1e-5
MASKED = -1e30
WSCALE = 64.0


class Chain:

    def __init__(self, eng, sem, per_round):
        self.eng, self.sem, self.per_round, self.base, self.n = eng, sem, per_round, 0, 0

    def begin(self, n):
        self.base, self.n = n * self.per_round, 0

    def mark(self, ins):
        self.n += 1
        ins.then_inc(self.sem, 1)

    def wait(self):
        self.eng.wait_ge(self.sem, self.base + self.n)

    def link(self, ins):
        self.mark(ins)
        self.wait()

    def end(self):
        assert self.n == self.per_round, (self.n, self.per_round)


def conv_moe_block(nc, x, conv_w1, conv_b1, conv_w2, conv_b2, conv_bias, Wg, bg, W1, b1, W2, b2, out):
    NIMG, C, HH, WW = x.shape
    PIX = HH * WW
    NBLK = PIX // P
    NTOK = NIMG * PIX
    E, D, H = W1.shape
    HS = H // P
    HALF = 512
    PW, PH = WW + 2, HH + 2
    assert C == P and D == P and NBLK * P == PIX
    NU, NB2 = NIMG // 2, 2 * NBLK
    assert NIMG % 8 == 0
    CENTER = TAPS // 2
    PE_TAPS = (CENTER, 1, 3, 5)
    DVE_TAPS = [k for k in range(TAPS) if k not in PE_TAPS]

    NPAIR = E * (E - 1) // 2
    UP_A = 2
    NUP = UP_A * (2 * E - UP_A - 1) // 2
    NREG = max(NUP, NPAIR - NUP)
    T = 2 * P
    TB = T // P
    CAP = NTOK + 2 * T
    OFF = [a * (2 * E - a - 1) // 2 for a in range(E - 1)]
    NT = NTOK // T + NPAIR
    NT_COLS = -(-NT // P)
    RW = D + 4
    W_LO, W_HI, ID = D, D + 1, D + 2
    TW, T_ROW, T_EXP, T_OFF = 8, 0, 1, 4
    O_1H, O_1L, O_2, O_B2 = 0, H, 2 * H, 4 * H
    EW = 4 * H + D
    assert NT % 4 == 0

    rows_dram = nc.dram_tensor("rows_by_pair", [NREG * CAP + T, RW], F32).ap()
    x1_dram = nc.dram_tensor("conv_out", [NIMG, P, PIX], F32).ap()
    y_dram = nc.dram_tensor("expert_out", [NTOK, D], F32).ap()
    tab_dram = nc.dram_tensor("tile_table", [NT_COLS * P, TW], I32).ap()

    x_v = x.rearrange("n c h w -> n c (h w)")
    out_v = out.rearrange("n c h w -> n c (h w)")
    row = lambda v, n: v.rearrange("(a n) -> a n", a=1)

    with ExitStack() as ctx:
        def sb(name, shape, dt=F32, held=ctx):
            return held.enter_context(nc.sbuf_tensor(name, shape, dt))

        def psum(name, cols):
            return ctx.enter_context(nc.psum_tensor(name, [P, cols], F32))

        def sem(name):
            return ctx.enter_context(nc.semaphore(name))

        ones = sb("ones", [P, P])
        mean_w = sb("mean_w", [P, P])
        centre_w = sb("centre_w", [P, P])
        ident = sb("ident", [P, P])
        tri = sb("tri", [P, P])
        tri_b = sb("tri_b", [P, P], BF16)
        ones_b = sb("ones_b", [P, P], BF16)
        eps_c = sb("eps_c", [P, 1])
        eps_t = sb("eps_t", [P, 1])
        desc = sb("desc", [P, E])
        pair_base = sb("pair_base", [P, NPAIR])
        tile_no = sb("tile_no", [P, NT_COLS])
        pad_rows = sb("pad_rows", [P, TB, RW])
        bias_sel = sb("bias_sel", [P, P], F16)

        stage = sb("stage", [P, E * H])
        wall = sb("wall", [P, E * EW], F16)
        wall_e = wall[:, :].rearrange("p (e w) -> p e w", w=EW)
        w2_e = wall_e[:, :, O_2:O_B2].rearrange("p e (s t d) -> p e s t d", s=HS, t=2)
        stage_1 = stage[:, :].rearrange("p (e h) -> p e h", e=E)
        stage_2 = stage[:, :].rearrange("p (e s d) -> p e s d", e=E, s=HS)
        b1col = sb("b1col", [P, E * HS])
        b1row = sb("b1row", [E * HS, P])
        b2st = sb("b2st", [P, E * D])
        b2_e = wall_e[:, :, O_B2:EW]
        b2low = sb("b2low", [P, E * D], F16)
        cw = sb("cw", [P, 2, TAPS * P])
        cwT = sb("cwT", [P, 2, TAPS, P])
        cb = sb("cb", [P, 2, TAPS])
        conv_b = sb("conv_b", [P, 1])
        wg = sb("wg", [P, E])
        wgc = sb("wgc", [P, E])
        bgrow = sb("bgrow", [1, E])
        bgb = sb("bgb", [P, E])

        psA = psum("psA", 1024)
        psV = psum("psV", 1024)
        psT = psum("psT", 1024)
        psG = psum("psG", 512)
        psR = psum("psR", 512)
        R_CNT, R_TAP = NB2 * NPAIR, (NB2 + 1) * NPAIR
        assert R_TAP + 4 * TAPS <= 512
        psVar, psConv = psV[:, 0:HALF], psV[:, HALF:2 * HALF]

        s_load = sem("weights_loaded")
        s_stage = sem("stage_loaded")
        s_const = sem("constants_made")
        s_setup_pe = sem("setup_products")
        s_setup_act = sem("setup_act")
        s_setup_dve = sem("setup_dve")
        x_in = [sem(f"x_in{j}") for j in range(4)]
        xc_ready, sq_ready, var_ready, ln_ready, sd_ready = map(sem, ("xc_ready", "sq_ready", "var_ready", "ln_ready", "sd_ready"))
        l_ready, max_ready, sum_ready = map(sem, ("l_ready", "max_ready", "sum_ready"))
        tap_ready, z_ready, ez_ready, taps_ready, diag_ready, conv_ready = map(
            sem, ("tap_ready", "z_ready", "ez_ready", "taps_ready", "diag_ready", "conv_ready"))
        x1_half = sem("x1_half")
        x1_out = [sem(f"x1_out{j}") for j in range(4)]
        tok_ready, stat_ready, tln_ready, rstd_ready, nmr_ready, xn_ready = map(
            sem, ("tok_ready", "stat_ready", "tln_ready", "rstd_ready", "nmr_ready", "xn_ready"))
        lg_ready, gap_ready, e2_ready, pairs_ready, rank_ready, idx_ready = map(
            sem, ("lg_ready", "gap_ready", "e2_ready", "pairs_ready", "rank_ready", "idx_ready"))
        rows_out = [sem(f"rows_out{p}") for p in range(2)]
        ch2, ch3, ch4, chb = map(sem, ("dve_s2", "dve_s3", "dve_s4", "dve_b"))
        tab_ready, tab_out, tab_in, padded = map(sem, ("tab_ready", "tab_out", "tab_in", "padded"))
        row_in = [sem(f"row_in{r}") for r in range(4)]
        y_out = [sem(f"y_out{r}") for r in range(4)]
        xT_ready, xh_done, xl_done, h_ready, g_done, hi0_done, hi1_done, lo_done, y_ready, ya_done, yt_done = map(
            sem, ("xT_ready", "xh_done", "xl_done", "h_ready", "g_done", "hi0_done", "hi1_done", "lo_done", "y_ready",
                  "ya_done", "yt_done"))
        yx_in = [sem(f"yx_in{q}") for q in range(2)]
        yT_ready, o_ready = sem("yT_ready"), sem("o_ready")
        o_out = [sem(f"o_out{q}") for q in range(2)]

        pooled = [sb(f"pooled{p}", [P, 2, 2]) for p in range(2)]
        zt, zm, z, zd, ez, taps = (sb(n, [P, TAPS, 2]) for n in ("zt", "zm", "z", "zd", "ez", "taps"))
        st = sb("st", [P, NBLK, 6])
        mv = sb("mv", [P, NBLK, 2])
        tln = sb("tln", [P, NBLK])
        rstd = sb("rstd", [P, NB2])
        nmr = sb("nmr", [P, NB2])
        lg, lg2, eq, sc, m1h, m2h, mh = (sb(n, [P, NB2, E]) for n in ("lg", "lg2", "eq", "sc", "m1h", "m2h", "mh"))
        m1, m2, s1, s2, gap, e2, den, wa, wb, flag, dw, fd, idf = (
            sb(n, [P, NB2]) for n in ("m1", "m2", "s1", "s2", "gap", "e2", "den", "wa", "wb", "flag", "dw", "fd", "idf"))
        pairs = sb("pairs", [P, NB2, NPAIR], BF16)
        pos = sb("pos", [P, NB2, NPAIR])
        base = sb("base", [P, NPAIR])
        idx = [sb(f"idx{p}", [P, NB2], I32) for p in range(2)]

        cnt, tiles_f, tend, zero28, ge, sel = (sb(n, [P, NPAIR]) for n in ("cnt", "tiles_f", "tend", "zero28", "ge", "sel"))
        cnt_i, tiles_i = sb("cnt_i", [P, NPAIR], I32), sb("tiles_i", [P, NPAIR], I32)
        base_i = sb("base_i", [P, NPAIR], I32)
        tp, tst, trow, ta, tb_, tt1, down_ = (sb(n, [P, NT_COLS]) for n in ("tp", "tst", "trow", "ta", "tb", "tt1", "grows_down"))
        tabt = sb("tabt", [P, NT_COLS, TW], I32)
        t_off = sb("t_off", [P, NT_COLS, 2])
        tab = sb("tab", [1, NT_COLS * P * TW], I32)

        phase_a = ExitStack()
        xb = [sb(f"xb{j}", [P, PIX], held=phase_a) for j in range(4)]
        sq = sb("sq", [P, PIX], held=phase_a)
        lnv = sb("lnv", [P, PIX], held=phase_a)
        sd = sb("sd", [P, PIX], held=phase_a)
        lp = [sb(f"lp{j}", [P, PH, PW], held=phase_a) for j in range(4)]
        x1 = [sb(f"x1_{j}", [P, PIX], held=phase_a) for j in range(4)]
        diag = [sb(f"diag{k}", [P, len(PE_TAPS), P], held=phase_a) for k in range(2)]
        rows = [sb(f"rows{p}", [P, NB2, RW], held=phase_a) for p in range(2)]
        phase_a.close()

        rt = [sb(f"rt{r}", [P, TB, RW]) for r in range(4)]
        xh = [sb(f"xh{q}", [P, T], F16) for q in range(2)]
        xl = [sb(f"xl{q}", [P, T], F16) for q in range(2)]
        g = [sb(f"g{q}", [P, HS * T]) for q in range(2)]
        gh = [sb(f"gh{q}", [P, HS * T], F16) for q in range(2)]
        gl = [sb(f"gl{q}", [P, HS * T], F16) for q in range(2)]
        ya = [sb(f"ya{r}", [P, TB, 2 * D]) for r in range(4)]
        yt = [sb(f"yt{r}", [P, TB, D]) for r in range(4)]

        ye = [sb(f"ye{q}", [P, NBLK, D]) for q in range(2)]
        xe = [sb(f"xe{q}", [P, PIX]) for q in range(2)]
        oe = [sb(f"oe{q}", [P, PIX]) for q in range(2)]

        inner = lambda j: lp[j][:, 1:1 + HH, 1:1 + WW]
        img = lambda t: t[:, :].rearrange("p (h w) -> p h w", w=WW)
        half_img = lambda t, h: img(t)[:, h * HH // 2:(h + 1) * HH // 2, :]
        spread = lambda t: t[:, :].unsqueeze(2).broadcast_to([P, NB2, E])
        per_blk = lambda t, n: t[:, :].unsqueeze(1).broadcast_to([P, NB2, n])

        FIRST, LAST = 4, NU - 2

        class Step:
            def __init__(self, t, r):
                self.t, self.r, self.fixed = t, r, isinstance(t, int)

            def on(self, stage):
                return not self.fixed or 0 <= 2 * self.t + self.r - (stage - 1) < NU

            def count(self, stage, per, more):
                return per * 2 * self.t + (per * (self.r - (stage - 1)) + more)

            def turns(self, stage):
                return self.t + (self.r - (stage - 1)) // 2

            def slot(self, stage):
                return (self.r - (stage - 1)) % 2

        def run_steps(eng, step):
            for s in range(FIRST):
                step(Step(s // 2, s % 2))
            with eng.Fori(FIRST // 2, LAST // 2, 1) as t:
                for r in range(2):
                    step(Step(t, r))
            for s in range(LAST, NU + 3):
                step(Step(s // 2, s % 2))

        hbank = (psV, psT)
        ybank = (psG, psR)

        block = ctx.enter_context(nc.Block())

        @block.sync
        def _(sp):
            for free in (*x1_out, *o_out):
                sp.sem_inc(free, 16)
            for dst, src in (
                (cw[:, 0, :], conv_w1.rearrange("(c k) j -> c (k j)", k=TAPS)),
                (cw[:, 1, :], conv_w2.rearrange("(c k) j -> c (k j)", k=TAPS)),
                (cb[:, 0, :], conv_b1.rearrange("(c k) -> c k", k=TAPS)),
                (cb[:, 1, :], conv_b2.rearrange("(c k) -> c k", k=TAPS)),
                (conv_b[:, :], conv_bias.rearrange("(c a) -> c a", a=1)),
                (wg[:, :], Wg), (bgrow[:, :], row(bg, E)),
                (b1row[:, :], b1.rearrange("e (s p) -> (e s) p", p=P)),
            ):
                sp.dma_start(dst, src).then_inc(s_load, 16)
            sp.dma_start(stage[:, :].rearrange("p (e h) -> p e h", e=E), W1.rearrange("e d h -> d e h")).then_inc(s_stage, 16)

            def load(n, q):
                sp.dma_start(xb[q][:, :], x_v[n] if isinstance(n, int) else x_v[bass.ds(n, 1)].rearrange("a c m -> (a c) m")).then_inc(x_in[q], 16)
            for j in range(4):
                load(j, j)
            sp.wait_ge(s_const, 1)
            b2_flat = b2.rearrange("(a e) d -> a (e d)", a=1)
            sp.dma_start(b2st[0:1, :], b2_flat).then_inc(s_load, 16)
            sp.dma_start(b2st[32:33, :], b2_flat).then_inc(s_load, 16)
            sp.wait_ge(s_setup_dve, 1)
            sp.dma_start(stage[:, :].rearrange("p (e s d) -> p e s d", e=E, s=HS), W2.rearrange("e (s p) d -> p e s d", p=P)).then_inc(s_stage, 16)

            def store(n, q):
                src = x1_dram[n] if isinstance(n, int) else x1_dram[bass.ds(n, 1)].rearrange("a c m -> (a c) m")
                sp.dma_start(src, x1[q][:, :]).then_inc(x1_out[q], 16)
            with sp.Fori(1, NIMG // 4, 1) as t:
                for j in range(4):
                    sp.wait_ge(x1_half, 8 * t + 2 * j - 6)
                    load(4 * t + j, j)
                    store(4 * t + j - 4, j)
            for j in range(4):
                sp.wait_ge(x1_half, 2 * (NIMG - 3 + j))
                store(NIMG - 4 + j, j)

            sp.wait_ge(tab_ready, 1)
            for k in range(NPAIR + 1):
                if k < NUP:
                    first = sp.value_load(base_i[0:1, k:k + 1], min_val=k * CAP, max_val=k * CAP + NTOK)
                elif k < NPAIR:
                    top = (k - NUP + 1) * CAP - 1
                    first = sp.value_load(base_i[0:1, k:k + 1], min_val=top - NTOK, max_val=top) - (T - 1)
                else:
                    first = NREG * CAP
                sp.dma_start(rows_dram[bass.ds(first, T), :].rearrange("(p b) f -> p b f", b=TB), pad_rows[:, :, :]).then_inc(padded, 16)
            sp.wait_ge(tab_ready, 2)
            sp.dma_start(tab_dram.rearrange("(c p) f -> p c f", p=P), tabt[:, :, :]).then_inc(tab_out, 16)
            for p in range(2):
                sp.wait_ge(rows_out[p], 16 * NB2 * (NU // 2))
            for j in range(4):
                sp.wait_ge(x1_out[j], 16 + 16 * (NIMG // 4))
            sp.wait_ge(tab_out, 16)
            sp.dma_start(tab[:, :], tab_dram.rearrange("(a n) f -> a (n f)", a=1)).then_inc(tab_in, 16)
            sp.wait_ge(tab_in, 16)

            sp.wait_ge(padded, 16 * (NPAIR + 1))
            def load_rows(first, r):
                sp.dma_start(rt[r][:, :, :], rows_dram[bass.ds(first, T), :].rearrange("(p b) f -> p b f", b=TB)).then_inc(row_in[r], 16)

            for r in range(4):
                first = sp.value_load(tab[0:1, TW * r:TW * r + 1], min_val=0, max_val=NREG * CAP)
                load_rows(first, r)
            with sp.Fori(1, NT // 4, 1) as t:
                for r in range(4):
                    first = sp.value_load(tab[0:1, bass.ds((4 * t + r) * TW, 1)], min_val=0, max_val=NREG * CAP)
                    sp.wait_ge(y_out[r], 16 * TB * t)
                    load_rows(first, r)

            for r in range(4):
                sp.wait_ge(y_out[r], 16 * TB * (NT // 4))
            with sp.Fori(0, NIMG // 2, 1) as t:
                for q in range(2):
                    n = 2 * t + q
                    sp.wait_ge(o_out[q], 16 + 16 * t)
                    sp.dma_start(ye[q][:, :, :], y_dram.rearrange("(n b p) d -> n p b d", b=NBLK, p=P)[bass.ds(n, 1)].rearrange("a p b d -> (a p) b d")).then_inc(yx_in[q], 16)
                    sp.dma_start(xe[q][:, :], x1_dram[bass.ds(n, 1)].rearrange("a c m -> (a c) m")).then_inc(yx_in[q], 16)
            for q in range(2):
                sp.wait_ge(o_out[q], 16 + 16 * (NIMG // 2))

        @block.gpsimd
        def _(pool):
            gp = nc.gpsimd
            gp.memset(b2st[:, :], 0.0).then_inc(s_const, 1)
            gp.memset(ones[:, :], 1.0)
            gp.memset(ones_b[:, :], 1.0)
            gp.memset(mean_w[:, :], 1.0 / C)
            gp.memset(eps_c[:, :], LN_C_EPS)
            gp.memset(eps_t[:, :], LN_T_EPS)
            gp.memset(bias_sel[:, :], 0.0)
            gp.memset(zero28[:, :], 0.0)
            for j in range(4):
                gp.memset(lp[j][:, :, :], 0.0)
            for p in range(2):
                gp.memset(rows[p][:, :, ID + 1], 0.0)
                gp.iota(rows[p][:, :, ID].bitcast(I32), [[P, NB2]], base=(2 * p - 4) * PIX, channel_multiplier=1)
            gp.memset(pad_rows[:, :, :], 0.0)
            gp.iota(desc[:, :], [[-1, E]], base=E, channel_multiplier=0, allow_small_or_imprecise_dtypes=True)
            gp.iota(tile_no[:, :], [[P, NT_COLS]], base=0, channel_multiplier=1, allow_small_or_imprecise_dtypes=True)
            gp.iota(pair_base[:, :], [[1, NPAIR]], base=0, channel_multiplier=0,
                    allow_small_or_imprecise_dtypes=True).then_inc(s_const, 1)
            pool.wait_ge(s_const, 2)
            gp.iota(pad_rows[:, :, ID].bitcast(I32), [[0, TB]], base=NTOK, channel_multiplier=1)
            gp.affine_select(out=ident[:, :], in_=ones[:, :], compare_op=ALU.is_equal, fill=0.0, base=0,
                             pattern=[[-1, P]], channel_multiplier=1)
            gp.affine_select(out=tri[:, :], in_=ones[:, :], compare_op=ALU.is_gt, fill=0.0, base=0,
                             pattern=[[1, P]], channel_multiplier=-1).then_inc(s_const, 1)

            routed = pool.alloc_register("routed")
            images = pool.alloc_register("images")
            tiles = pool.alloc_register("tiles")
            for reg in (routed, images, tiles):
                pool.reg_mov(reg, 0)

            with pool.Fori(0, NU // 2, 1) as t:
                for p in range(2):
                    pool.reg_alu(routed, routed, 1, ALU.add)
                    pool.reg_alu(images, images, 2, ALU.add)
                    pool.wait_ge(s_const, 3)
                    pool.wait_ge(idx_ready, routed)
                    pool.wait_ge(xn_ready, images)
                    for b in range(NB2):
                        gp.indirect_dma_start(rows_dram, bass.IndirectOffsetOnAxis(ap=idx[p][:, b:b + 1].bitcast(U32), axis=0),
                                              rows[p][:, b, :], None).then_inc(rows_out[p], 16)

            with pool.Fori(0, NT // 4, 1) as t:
                for r in range(4):
                    pool.wait_ge(ya_done, 2 * (4 * t + r) + 4)
                    gp.tensor_tensor(yt[r][:, :, :], ya[r][:, :, 0:D], ya[r][:, :, D:2 * D], ALU.add).then_inc(yt_done, 1)
                    pool.reg_alu(tiles, tiles, 1, ALU.add)
                    pool.wait_ge(s_const, 3)
                    pool.wait_ge(yt_done, tiles)
                    for b in range(TB):
                        gp.indirect_dma_start(y_dram, bass.IndirectOffsetOnAxis(ap=rt[r][:, b, ID:ID + 1].bitcast(U32), axis=0),
                                              yt[r][:, b, :], None, bounds_check=NTOK - 1, oob_is_err=False).then_inc(y_out[r], 16)

        @block.scalar
        def _(act):
            sc_ = nc.scalar
            act.wait_ge(s_stage, 16)
            sc_.activation(wall_e[:, :, O_1H:O_1L], stage_1, ACT.Copy, scale=WSCALE).then_inc(s_setup_act, 1)
            act.wait_ge(s_load, 16 * 10)
            sc_.activation(b2_e, b2st[:, :].rearrange("p (e d) -> p e d", e=E), ACT.Copy, scale=WSCALE).then_inc(s_setup_act, 1)
            for n in range(5):
                act.wait_ge(s_setup_pe, n + 1)
                k = min(4, 2 * TAPS - 4 * n)
                sc_.activation(cwT[:, :, :, :].rearrange("p a k c -> p (a k) c")[:, 4 * n:4 * n + k, :],
                               (psA if n % 2 == 0 else psV)[:, 0:k * P].rearrange("p (k c) -> p k c", c=P), ACT.Copy).then_inc(s_setup_act, 1)
            act.wait_ge(s_setup_pe, 6)
            sc_.activation(b1col[:, :], psG[:, 0:E * HS], ACT.Copy).then_inc(s_setup_act, 1)
            sc_.activation(bgb[:, :], psG[:, 64:64 + E], ACT.Copy).then_inc(s_setup_act, 1)
            act.wait_ge(s_stage, 32)
            for e in range(E):
                last = sc_.activation(w2_e[:, e, :, 0, :], stage_2[:, e, :, :], ACT.Copy, scale=WSCALE)
            last.then_inc(s_setup_act, 1)
            act.wait_ge(s_const, 3)

            def square(st_, k):
                act.wait_ge(xc_ready, st_.count(1, 2, k + 1))
                if not st_.fixed or st_.t + st_.r + k > 0:
                    act.wait_ge(sum_ready, st_.count(1, 2, k))
                sc_.activation(sq[:, :], psA[:, :], ACT.Square).then_inc(sq_ready, 1)

            def inv_std(st_, k, h):
                cols = slice(h * HALF, (h + 1) * HALF)
                n = st_.count(1, 4, 2 * k + h + 1)
                act.wait_ge(var_ready, n)
                sc_.activation(lnv[:, cols], psVar, ACT.Ln, bias=eps_c[:, :]).then_inc(ln_ready, 1)
                act.wait_ge(ln_ready, n)
                if not st_.fixed or st_.t + st_.r + k > 0:
                    act.wait_ge(l_ready, st_.count(1, 2, k))
                sc_.activation(sd[:, cols], lnv[:, cols], ACT.Exp, scale=-0.5).then_inc(sd_ready, 1)

            def sum_up(st_, k):
                act.wait_ge(l_ready, st_.count(1, 2, k + 1))
                sc_.activation(img(sq), inner(2 * st_.slot(1) + k), ACT.Copy, accum_out=pooled[st_.slot(1)][:, 0, k:k + 1]).then_inc(sum_ready, 1)

            def diagonals(st_, k):
                act.wait_ge(taps_ready, st_.count(2, 1, 1))
                if not st_.fixed or 2 * st_.t + st_.r > 1:
                    act.wait_ge(conv_ready, st_.count(2, 4, 2 * k - 2))
                for m, tap in enumerate(PE_TAPS):
                    last = sc_.activation(diag[k][:, m, :], ident[:, :], ACT.Copy, scale=taps[:, tap, k:k + 1])
                last.then_inc(diag_ready, 1)

            def token_std(st_, k):
                n = st_.count(3, 2, k + 1)
                act.wait_ge(stat_ready, n)
                sc_.activation(tln[:, :], mv[:, :, 1], ACT.Ln, bias=eps_t[:, :]).then_inc(tln_ready, 1)
                act.wait_ge(tln_ready, n)
                sc_.activation(rstd[:, k * NBLK:(k + 1) * NBLK], tln[:, :], ACT.Exp, scale=-0.5).then_inc(rstd_ready, 1)

            def normalise(st_, k):
                p = st_.slot(3)
                act.wait_ge(nmr_ready, st_.count(3, 2, k + 1))
                if not st_.fixed or st_.turns(3) > 0:
                    act.wait_ge(rows_out[p], 16 * NB2 * st_.turns(3))
                for b in range(NBLK):
                    bk = k * NBLK + b
                    last = sc_.activation(rows[p][:, bk, 0:D], psT[:, b * P:(b + 1) * P], ACT.Identity,
                                          bias=nmr[:, bk:bk + 1], scale=rstd[:, bk:bk + 1])
                last.then_inc(xn_ready, 1)

            def step(st_):
                if st_.on(1):
                    square(st_, 0)
                if st_.on(4):
                    act.wait_ge(gap_ready, st_.count(4, 1, 1))
                    sc_.activation(e2[:, :], gap[:, :], ACT.Exp).then_inc(e2_ready, 1)
                if st_.on(2):
                    act.wait_ge(z_ready, st_.count(2, 1, 1))
                    sc_.activation(ez[:, :, :], zd[:, :, :], ACT.Exp).then_inc(ez_ready, 1)
                    diagonals(st_, 0)
                for k in range(2):
                    if st_.on(1):
                        if k == 1:
                            square(st_, 1)
                        inv_std(st_, k, 0)
                    if st_.on(3):
                        token_std(st_, k)
                    if st_.on(1):
                        inv_std(st_, k, 1)
                    if st_.on(3):
                        normalise(st_, k)
                    if k == 0 and st_.on(2):
                        diagonals(st_, 1)
                    if st_.on(1):
                        sum_up(st_, k)

            run_steps(act, step)

            act.wait_ge(tab_in, 16)

            def high(j, q):
                act.wait_ge(xT_ready, j + 1)
                sc_.activation(xh[q][:, :], psA[:, 512 * q:512 * q + T], ACT.Copy).then_inc(xh_done, 1)

            def gelu(j, side):
                at = TW * j + T_EXP + side
                e = act.value_load(tab[0:1, at:at + 1] if isinstance(j, int) else tab[0:1, bass.ds(at, 1)], min_val=0, max_val=E - 1)
                act.wait_ge(h_ready, 2 * j + side + 1)
                if not isinstance(j, int) or j >= 1:
                    act.wait_ge(lo_done, 2 * j + side - 1)
                for s in range(HS):
                    last = sc_.activation(g[side][:, s * T:(s + 1) * T], hbank[side][:, s * T:(s + 1) * T], ACT.Gelu,
                                          bias=b1col[:, bass.ds(e * HS + s, 1)], scale=1.0 / WSCALE)
                last.then_inc(g_done, 1)
                if side == 1:
                    act.wait_ge(g_done, 2 * j + 2)
                    if not isinstance(j, int) or j >= 1:
                        act.wait_ge(y_ready, 2 * j)
                    sc_.activation(gh[1][:, :], g[1][:, :], ACT.Copy).then_inc(hi1_done, 1)

            high(0, 0)
            high(1, 1)
            gelu(0, 0)
            gelu(0, 1)

            def dstep(j, r):
                if not isinstance(j, int) or j + 1 < NT:
                    gelu(j + 1, 0)
                if not isinstance(j, int) or j + 2 < NT:
                    high(j + 2, r % 2)
                if not isinstance(j, int) or j + 1 < NT:
                    gelu(j + 1, 1)
            with act.Fori(0, NT // 4 - 1, 1) as t:
                for r in range(4):
                    dstep(4 * t + r, r)
            for r in range(4):
                dstep(NT - 4 + r, r)

            with act.Fori(0, NIMG // 2, 1) as t:
                for q in range(2):
                    act.wait_ge(o_ready, 2 * t + q + 3)
                    act.dma_start(out_v[bass.ds(2 * t + q, 1)].rearrange("a c m -> (a c) m"), oe[q][:, :]).then_inc(o_out[q], 16)

        @block.tensor
        def _(pe):
            te = nc.tensor
            pe.wait_ge(s_const, 3)
            pe.wait_ge(s_load, 16 * 10)
            for n in range(5):
                k = min(4, 2 * TAPS - 4 * n)
                if n >= 2:
                    pe.wait_ge(s_setup_act, 2 + n - 1)
                for m in range(k):
                    a, tap = divmod(4 * n + m, TAPS)
                    last = te.transpose((psA if n % 2 == 0 else psV)[:, m * P:(m + 1) * P], cw[:, a, tap * P:(tap + 1) * P], ident[:, :])
                last.then_inc(s_setup_pe, 1)
            te.transpose(psG[:, 0:E * HS], b1row[:, :], ident[0:E * HS, 0:E * HS])
            te.matmul(psG[:, 64:64 + E], ones[0:1, :], bgrow[:, :], start=True, stop=True)
            te.matmul(psG[:, 128:128 + E], mean_w[:, :], wg[:, :], start=True, stop=True).then_inc(s_setup_pe, 1)
            pe.wait_ge(s_setup_act, 9)
            pe.wait_ge(s_setup_dve, 3)

            def centre(st_, k):
                j = 2 * st_.slot(1) + k
                pe.wait_ge(x_in[j], 16 * (st_.turns(1) + 1))
                if not st_.fixed or st_.t + st_.r + k > 0:
                    pe.wait_ge(l_ready, st_.count(1, 2, k))
                for h in range(2):
                    last = te.matmul(psA[:, h * HALF:(h + 1) * HALF], centre_w[:, :], xb[j][:, h * HALF:(h + 1) * HALF], start=True, stop=True)
                last.then_inc(xc_ready, 1)

            def variance(st_, k, h):
                if h == 0:
                    pe.wait_ge(sq_ready, st_.count(1, 2, k + 1))
                if not st_.fixed or st_.t + st_.r + k + h > 0:
                    pe.wait_ge(ln_ready, st_.count(1, 4, 2 * k + h))
                te.matmul(psVar, mean_w[:, :], sq[:, h * HALF:(h + 1) * HALF], start=True, stop=True).then_inc(var_ready, 1)

            def tap_logits(st_):
                pe.wait_ge(sum_ready, st_.count(2, 2, 2))
                pe.wait_ge(max_ready, st_.count(2, 2, 2))
                if not st_.fixed or 2 * st_.t + st_.r > 3:
                    pe.wait_ge(idx_ready, st_.count(4, 1, 0))
                for a in range(2):
                    for tap in range(TAPS):
                        at = R_TAP + 2 * (a * TAPS + tap)
                        last = te.matmul(psR[:, at:at + 2], cwT[:, a, tap, :], pooled[st_.slot(2)][:, a, :], start=True, stop=True)
                last.then_inc(tap_ready, 1)

            def turn(st_, k):
                j = 2 * st_.slot(3) + k
                pe.wait_ge(x1_half, st_.count(3, 4, 2 * k + 2))
                if k == 0 and (not st_.fixed or st_.count(3, 1, 0) > 0):
                    pe.wait_ge(lg_ready, st_.count(3, 1, 0))
                if not st_.fixed or st_.count(3, 2, k) > 0:
                    pe.wait_ge(xn_ready, st_.count(3, 2, k))
                for b in range(NBLK):
                    te.transpose(psT[:, b * P:(b + 1) * P], x1[j][:, b * P:(b + 1) * P], ident[:, :])
                    at = (k * NBLK + b) * E
                    last = te.matmul(psG[:, at:at + E], x1[j][:, b * P:(b + 1) * P], wgc[:, :], start=True, stop=True)
                last.then_inc(tok_ready, 1)

            def conv(st_, k, h):
                j = 2 * st_.slot(2) + k
                if h == 0:
                    pe.wait_ge(diag_ready, st_.count(2, 2, k + 1))
                if not st_.fixed or st_.count(2, 4, 2 * k + h) > 0:
                    pe.wait_ge(x1_half, st_.count(2, 4, 2 * k + h))
                for m, tap in enumerate(PE_TAPS):
                    dy, dx = divmod(tap, 3)
                    y = dy + h * HH // 2
                    last = te.matmul(psConv.rearrange("p (h w) -> p h w", w=WW), diag[k][:, m, :], lp[j][:, y:y + HH // 2, dx:dx + WW],
                                     start=(m == 0), stop=(m == len(PE_TAPS) - 1))
                last.then_inc(conv_ready, 1)

            def ranks(st_):
                pe.wait_ge(pairs_ready, st_.count(4, 1, 1))
                if st_.on(2):
                    pe.wait_ge(z_ready, st_.count(2, 1, 1))
                elif st_.count(4, 1, 0) > 0:
                    pe.wait_ge(idx_ready, st_.count(4, 1, 0))
                n = NPAIR
                te.matmul(psR[:, 0:R_CNT], tri_b[:, :], pairs[:, :, :].rearrange("p b k -> p (b k)"), start=True, stop=False, skip_group_check=True)
                for b in range(NB2):
                    left = NB2 - b
                    last = te.matmul(psR[:, (b + 1) * n:(NB2 + 1) * n].rearrange("p (b k) -> p b k", k=n), ones_b[:, :],
                                     pairs[:, b:b + 1, :].broadcast_to([P, left, n]), start=False, stop=(b == NB2 - 1), skip_group_check=True)
                last.then_inc(rank_ready, 1)

            def step(st_):
                for k in range(2):
                    if st_.on(3):
                        turn(st_, k)
                    if k == 0 and st_.on(2):
                        tap_logits(st_)
                    if st_.on(1):
                        if st_.fixed and st_.t + st_.r + k == 0:
                            centre(st_, 0)
                        variance(st_, k, 0)
                    if k == 0 and st_.on(4):
                        ranks(st_)
                    if st_.on(2):
                        conv(st_, k, 0)
                    if st_.on(1):
                        variance(st_, k, 1)
                    if st_.on(2):
                        conv(st_, k, 1)
                    following = Step(st_.t + st_.r, 1 - st_.r)
                    if k == 0 and st_.on(1):
                        centre(st_, 1)
                    if k == 1 and (not st_.fixed or 2 * st_.t + st_.r + 1 < NU):
                        centre(following, 0)

            run_steps(pe, step)

            pe.wait_ge(tab_in, 16)
            pe.wait_ge(idx_ready, NU)

            off = [[pe.alloc_register(f"off{q}{side}") for side in range(2)] for q in range(2)]

            def experts(j, q):
                at = TW * j + T_OFF
                pe.load(off[q], tab[0:1, at:at + 2] if isinstance(j, int) else tab[0:1, bass.ds(at, 2)])

            def weights(q, side):
                return pe.snap(off[q][side], min_val=0, max_val=(E - 1) * EW)

            def turn_rows(j, r, t):
                pe.wait_ge(row_in[r], 16 * (t + 1))
                if not isinstance(j, int) or j >= 2:
                    pe.wait_ge(xl_done, j - 1)
                    pe.wait_ge(xh_done, j - 1)
                for b in range(TB):
                    last = te.transpose(psA[:, 512 * (r % 2) + b * P:512 * (r % 2) + (b + 1) * P], rt[r][:, b, 0:D], ident[:, :])
                last.then_inc(xT_ready, 1)

            def up(j, side, q):
                w = weights(q, side)
                pe.wait_ge(xh_done, j + 1)
                pe.wait_ge(xl_done, j + 1)
                if not isinstance(j, int) or j >= 1:
                    pe.wait_ge(g_done, 2 * j + side - 1)
                for s in range(HS):
                    o = hbank[side][:, s * T:(s + 1) * T]
                    high = wall[:, bass.ds(w + (O_1H + s * P), P)]
                    te.matmul(o, high, xh[q][:, :], start=True, stop=False)
                    te.matmul(o, high, xl[q][:, :], start=False, stop=False)
                    last = te.matmul(o, wall[:, bass.ds(w + (O_1L + s * P), P)], xh[q][:, :], start=False, stop=True)
                last.then_inc(h_ready, 1)

            def down(j, side, q):
                w = weights(q, side)
                pe.wait_ge(lo_done, 2 * j + side + 1)
                pe.wait_ge((hi0_done, hi1_done)[side], j + 1)
                pe.wait_ge(ya_done, 2 * j + side + 1)
                bank = ybank[side]
                for s in range(HS):
                    both = wall[:, bass.ds(w + (O_2 + 2 * s * D), 2 * D)]
                    high = wall[:, bass.ds(w + (O_2 + 2 * s * D), D)]
                    for b in range(TB):
                        lhs = slice(s * T + b * P, s * T + (b + 1) * P)
                        te.matmul(bank[:, 2 * b * D:2 * (b + 1) * D], gh[side][:, lhs], both, start=(s == 0 and b == 0), stop=False, skip_group_check=True)
                        te.matmul(bank[:, 2 * b * D:(2 * b + 1) * D], gl[side][:, lhs], high, start=False, stop=False, skip_group_check=True)
                bias = wall[:, bass.ds(w + O_B2, D)]
                for b in range(TB):
                    last = te.matmul(bank[:, 2 * b * D:(2 * b + 1) * D], bias_sel[:, :], bias, start=False, stop=(b == TB - 1), skip_group_check=True)
                last.then_inc(y_ready, 1)

            experts(0, 0)
            turn_rows(0, 0, 0)
            turn_rows(1, 1, 0)
            up(0, 0, 0)
            up(0, 1, 0)

            def dstep(j, r, t):
                more, q = not isinstance(j, int), r % 2
                if more or j + 1 < NT:
                    experts(j + 1, 1 - q)
                    up(j + 1, 0, 1 - q)
                if more or j + 2 < NT:
                    turn_rows(j + 2, (r + 2) % 4, t + (r + 2) // 4)
                down(j, 0, q)
                if more or j + 1 < NT:
                    up(j + 1, 1, 1 - q)
                down(j, 1, q)
            with pe.Fori(0, NT // 4 - 1, 1) as t:
                for r in range(4):
                    dstep(4 * t + r, r, t)
            for r in range(4):
                dstep(NT - 4 + r, r, NT // 4 - 1)

            with pe.Fori(0, NIMG // 2, 1) as t:
                for q in range(2):
                    pe.wait_ge(yx_in[q], 32 * (t + 1))
                    pe.wait_ge(o_ready, 2 * t + q + 1)
                    for b in range(NBLK):
                        last = te.transpose((psA if q == 0 else psV)[:, b * P:(b + 1) * P], ye[q][:, b, :], ident[:, :])
                    last.then_inc(yT_ready, 1)

        @block.vector
        def _(dve):
            v = nc.vector
            dve.wait_ge(s_setup_act, 1)
            v.scalar_tensor_tensor(out=wall_e[:, :, O_1L:O_2], in0=stage_1, scalar=WSCALE, in1=wall_e[:, :, O_1H:O_1L], op0=ALU.mult, op1=ALU.subtract).then_inc(s_setup_dve, 1)
            dve.wait_ge(s_const, 3)
            v.memset(bias_sel[0:1, :], 1.0)
            v.memset(bias_sel[32:33, :], 1.0)
            v.tensor_copy(tri_b[:, :], tri[:, :])
            v.tensor_tensor(centre_w[:, :], ident[:, :], mean_w[:, :], ALU.subtract)
            v.tensor_scalar(pair_base[:, 0:NUP], pair_base[:, 0:NUP], float(CAP), None, ALU.mult)
            v.tensor_scalar(pair_base[:, NUP:NPAIR], pair_base[:, NUP:NPAIR], float(CAP), float(CAP * (1 - NUP) - 1), ALU.mult, ALU.add).then_inc(s_setup_dve, 1)
            dve.wait_ge(s_setup_dve, 2)
            v.tensor_copy(base[:, :], pair_base[:, :])
            dve.wait_ge(s_setup_act, 2)
            v.scalar_tensor_tensor(out=b2low[:, :].rearrange("p (e d) -> p e d", e=E), in0=b2st[:, :].rearrange("p (e d) -> p e d", e=E), scalar=WSCALE, in1=b2_e, op0=ALU.mult, op1=ALU.subtract)
            dve.wait_ge(s_setup_act, 9)
            v.tensor_tensor(wgc[:, :], wg[:, :], psG[:, 128:128 + E], ALU.subtract).then_inc(s_setup_dve, 1)
            dve.wait_ge(s_setup_dve, 3)
            v.tensor_copy(b2_e[32:33], b2low[32:33, :].rearrange("p (e d) -> p e d", e=E)).then_inc(s_setup_dve, 1)
            dve.wait_ge(s_setup_act, 10)
            for e in range(E):
                last = v.scalar_tensor_tensor(out=w2_e[:, e, :, 1, :], in0=stage_2[:, e, :, :], scalar=WSCALE, in1=w2_e[:, e, :, 0, :], op0=ALU.mult, op1=ALU.subtract)
            last.then_inc(s_setup_dve, 1)

            after_stats = dve.alloc_register("after_stats")
            c2 = Chain(dve, ch2, 6 + 2 * len(DVE_TAPS))
            c3 = Chain(dve, ch3, 2)
            c4 = Chain(dve, ch4, 27)

            def norm(st_, k):
                j = 2 * st_.slot(1) + k
                n = st_.count(1, 2, k + 1)
                dve.wait_ge(sd_ready, st_.count(1, 4, 2 * k + 2))
                v.tensor_tensor(inner(j), img(psA), img(sd), ALU.mult).then_inc(l_ready, 1)
                dve.wait_ge(l_ready, n)
                v.tensor_reduce(pooled[st_.slot(1)][:, 1, k:k + 1], inner(j), mybir.AxisListType.XY, ALU.max).then_inc(max_ready, 1)

            def tap_softmax(st_):
                link = c2.link
                c2.begin(st_.count(2, 1, 0))
                prod = lambda a: psR[:, R_TAP + 2 * a * TAPS:R_TAP + 2 * (a + 1) * TAPS].rearrange("p (t k) -> p t k", k=2)
                both = lambda t: t.unsqueeze(2).broadcast_to([P, TAPS, 2])
                dve.wait_ge(tap_ready, st_.count(2, 1, 1))
                v.scalar_tensor_tensor(out=zt[:, :, :], in0=prod(0), scalar=1.0 / PIX, in1=both(cb[:, 0, :]), op0=ALU.mult, op1=ALU.add)
                link(v.tensor_tensor(zm[:, :, :], prod(1), both(cb[:, 1, :]), ALU.add))
                link(v.tensor_tensor(z[:, :, :], zm[:, :, :], zt[:, :, :], ALU.subtract))
                link(v.tensor_reduce(zt[:, :, :], z[:, :, :].unsqueeze(3), AX_X, ALU.max))
                v.tensor_tensor(zd[:, :, :], z[:, :, :], zt[:, :, :], ALU.subtract).then_inc(z_ready, 1)
                dve.wait_ge(ez_ready, st_.count(2, 1, 1))
                link(v.tensor_reduce(zm[:, :, :], ez[:, :, :].unsqueeze(3), AX_X, ALU.add))
                link(v.reciprocal(zt[:, :, :], zm[:, :, :]))
                link(v.tensor_tensor(taps[:, :, :], ez[:, :, :], zt[:, :, :], ALU.mult))
                v.tensor_scalar(taps[:, CENTER, :], taps[:, CENTER, :], 1.0, None, ALU.add).then_inc(taps_ready, 1)

            def window(st_, k):
                j = 2 * st_.slot(2) + k
                dve.wait_ge(taps_ready, st_.count(2, 1, 1))
                dve.wait_ge(x1_out[j], 16 + 16 * st_.turns(2))
                for m, tap in enumerate(DVE_TAPS):
                    dy, dx = divmod(tap, 3)
                    c2.link(v.scalar_tensor_tensor(out=img(x1[j]), in0=lp[j][:, dy:dy + HH, dx:dx + WW], scalar=taps[:, tap, k:k + 1],
                                                   in1=img(xb[j] if m == 0 else x1[j]), op0=ALU.mult, op1=ALU.add))

            def join(st_, k, h):
                j = 2 * st_.slot(2) + k
                cols = slice(h * HALF, (h + 1) * HALF)
                dve.wait_ge(conv_ready, st_.count(2, 4, 2 * k + h + 1))
                v.scalar_tensor_tensor(out=x1[j][:, cols], in0=psConv, scalar=conv_b[:, :], in1=x1[j][:, cols], op0=ALU.add, op1=ALU.add).then_inc(x1_half, 1)

            def statistics(st_, k):
                if k == 0:
                    c3.begin(st_.count(3, 1, 0))
                dve.wait_ge(tok_ready, st_.count(3, 2, k + 1))
                for b in range(NBLK):
                    last = v.bn_stats(st[:, b, :], psT[:, b * P:(b + 1) * P])
                c3.mark(last)
                dve.reg_mov(after_stats, c3.base + c3.n)
                dve.wait_ge(s_const, 3)
                dve.wait_ge(ch3, after_stats)
                for b in range(NBLK):
                    last = v.bn_aggr(mv[:, b, :], st[:, b, :])
                last.then_inc(stat_ready, 1)

            def shifts(st_, k):
                blks = slice(k * NBLK, (k + 1) * NBLK)
                dve.wait_ge(rstd_ready, st_.count(3, 2, k + 1))
                v.scalar_tensor_tensor(out=nmr[:, blks], in0=mv[:, :, 0], scalar=-1.0, in1=rstd[:, blks], op0=ALU.mult, op1=ALU.mult).then_inc(nmr_ready, 1)
                if k == 1:
                    v.tensor_tensor(lg[:, :, :], psG[:, 0:NB2 * E].rearrange("p (b e) -> p b e", e=E), spread(rstd), ALU.mult).then_inc(lg_ready, 1)

            def choose(st_):
                link = c4.link
                c4.begin(st_.count(4, 1, 0))
                dve.wait_ge(lg_ready, st_.count(4, 1, 1))
                link(v.tensor_tensor(lg[:, :, :], lg[:, :, :], per_blk(bgb, E), ALU.add))
                for n, (src, mx, s, mask) in enumerate(((lg, m1, s1, m1h), (lg2, m2, s2, m2h))):
                    if n == 1:
                        link(v.scalar_tensor_tensor(out=lg2[:, :, :], in0=m1h[:, :, :], scalar=MASKED, in1=lg[:, :, :], op0=ALU.mult, op1=ALU.add))
                    link(v.tensor_reduce(mx[:, :], src[:, :, :], AX_X, ALU.max))
                    link(v.tensor_tensor(eq[:, :, :], src[:, :, :], spread(mx), ALU.is_equal))
                    link(v.tensor_tensor(sc[:, :, :], eq[:, :, :], per_blk(desc, E), ALU.mult))
                    link(v.tensor_reduce(s[:, :], sc[:, :, :], AX_X, ALU.max))
                    link(v.tensor_tensor(mask[:, :, :], sc[:, :, :], spread(s), ALU.is_equal))
                v.tensor_tensor(gap[:, :], m2[:, :], m1[:, :], ALU.subtract).then_inc(gap_ready, 1)
                link(v.tensor_tensor(mh[:, :, :], m1h[:, :, :], m2h[:, :, :], ALU.add))
                for a in range(E - 1):
                    n = E - 1 - a
                    last = v.scalar_tensor_tensor(out=pairs[:, :, OFF[a]:OFF[a] + n], in0=mh[:, :, a + 1:E], scalar=1.0 if a < UP_A else -1.0,
                                                  in1=mh[:, :, a:a + 1].broadcast_to([P, NB2, n]), op0=ALU.mult, op1=ALU.mult)
                last.then_inc(pairs_ready, 1)

            def weigh(st_):
                link = c4.link
                r_ = rows[st_.slot(4)]
                dve.wait_ge(e2_ready, st_.count(4, 1, 1))
                link(v.tensor_scalar(den[:, :], e2[:, :], WSCALE, WSCALE, ALU.mult, ALU.add))
                link(v.reciprocal(wa[:, :], den[:, :]))
                link(v.tensor_tensor(wb[:, :], e2[:, :], wa[:, :], ALU.mult))
                link(v.tensor_tensor(flag[:, :], s1[:, :], s2[:, :], ALU.is_gt))
                link(v.tensor_tensor(dw[:, :], wa[:, :], wb[:, :], ALU.subtract))
                link(v.tensor_tensor(fd[:, :], flag[:, :], dw[:, :], ALU.mult))
                dve.wait_ge(xn_ready, st_.count(4, 2, 2))
                link(v.tensor_tensor(r_[:, :, W_LO], wb[:, :], fd[:, :], ALU.add))
                link(v.tensor_tensor(r_[:, :, W_HI], wa[:, :], fd[:, :], ALU.subtract))
                link(v.tensor_scalar(r_[:, :, ID].bitcast(I32), r_[:, :, ID].bitcast(I32), 4 * PIX, None, ALU.add))

            def place(st_):
                link = c4.link
                dve.wait_ge(rank_ready, st_.count(4, 1, 1))
                dve.wait_ge(pairs_ready, st_.count(4, 1, 1))
                link(v.tensor_tensor(pos[:, :, :], psR[:, 0:R_CNT].rearrange("p (b k) -> p b k", k=NPAIR), per_blk(base, NPAIR), ALU.add))
                link(v.tensor_tensor(pos[:, :, :], pos[:, :, :], pairs[:, :, :], ALU.mult))
                link(v.tensor_reduce(idf[:, :], pos[:, :, :], AX_X, ALU.add))
                link(v.tensor_tensor(base[:, :], base[:, :], psR[:, R_CNT:R_CNT + NPAIR], ALU.add))
                link(v.scalar_tensor_tensor(out=idf[:, :], in0=idf[:, :], scalar=-1.0, in1=idf[:, :], op0=ALU.mult, op1=ALU.max))
                v.tensor_copy(idx[st_.slot(4)][:, :], idf[:, :]).then_inc(idx_ready, 1)
                c4.end()

            def step(st_):
                if st_.on(4):
                    choose(st_)
                if st_.on(2):
                    tap_softmax(st_)
                if st_.on(4):
                    weigh(st_)
                for k in range(2):
                    if st_.on(3):
                        statistics(st_, k)
                    if st_.on(2):
                        window(st_, k)
                    if st_.on(3):
                        shifts(st_, k)
                    if st_.on(2):
                        join(st_, k, 0)
                    if st_.on(1):
                        norm(st_, k)
                    if st_.on(2):
                        join(st_, k, 1)
                    if k == 0 and st_.on(4):
                        place(st_)

            run_steps(dve, step)

            cb_ = Chain(dve, chb, 0)
            link = cb_.link
            dve.wait_ge(idx_ready, NU)
            v.tensor_copy(base_i[:, :], base[:, :]).then_inc(tab_ready, 1)
            link(v.tensor_tensor(cnt[:, :], base[:, :], pair_base[:, :], ALU.subtract))
            link(v.scalar_tensor_tensor(out=cnt[:, :], in0=cnt[:, :], scalar=-1.0, in1=cnt[:, :], op0=ALU.mult, op1=ALU.max))
            link(v.tensor_scalar(cnt[:, :], cnt[:, :], float(T - 1), None, ALU.add))
            link(v.tensor_copy(cnt_i[:, :], cnt[:, :]))
            link(v.tensor_scalar(tiles_i[:, :], cnt_i[:, :], T.bit_length() - 1, None, ALU.arith_shift_right))
            link(v.tensor_copy(tiles_f[:, :], tiles_i[:, :]))
            link(v.tensor_tensor_scan(tend[:, :], tiles_f[:, :], zero28[:, :], 0.0, ALU.add, ALU.add))
            for c in range(NT_COLS):
                link(v.tensor_scalar(ge[:, :], tend[:, :], tile_no[:, c:c + 1], None, ALU.is_le))
                link(v.tensor_reduce(tp[:, c:c + 1], ge[:, :], AX_X, ALU.add))
                link(v.tensor_tensor(sel[:, :], ge[:, :], tend[:, :], ALU.mult))
                link(v.tensor_reduce(tst[:, c:c + 1], sel[:, :], AX_X, ALU.max))
            link(v.tensor_scalar(trow[:, :], tp[:, :], float(CAP), None, ALU.mult))
            link(v.tensor_tensor(tt1[:, :], tile_no[:, :], tst[:, :], ALU.subtract))
            link(v.scalar_tensor_tensor(out=trow[:, :], in0=tt1[:, :], scalar=float(T), in1=trow[:, :], op0=ALU.mult, op1=ALU.add))
            link(v.tensor_scalar(down_[:, :], tp[:, :], float(NUP), None, ALU.is_ge))
            link(v.tensor_tensor(tt1[:, :], tt1[:, :], down_[:, :], ALU.mult))
            link(v.scalar_tensor_tensor(out=trow[:, :], in0=tt1[:, :], scalar=float(-2 * T), in1=trow[:, :], op0=ALU.mult, op1=ALU.add))
            link(v.scalar_tensor_tensor(out=trow[:, :], in0=down_[:, :], scalar=float(CAP - T - NUP * CAP), in1=trow[:, :], op0=ALU.mult, op1=ALU.add))
            link(v.tensor_scalar(trow[:, :], trow[:, :], float(NREG * CAP), None, ALU.min))
            link(v.memset(ta[:, :], 0.0))
            link(v.tensor_scalar(tb_[:, :], tp[:, :], 1.0, None, ALU.add))
            for s in range(1, E - 1):
                link(v.tensor_scalar(tt1[:, :], tp[:, :], float(OFF[s]), None, ALU.is_ge))
                link(v.tensor_tensor(ta[:, :], ta[:, :], tt1[:, :], ALU.add))
                link(v.scalar_tensor_tensor(out=tb_[:, :], in0=tt1[:, :], scalar=float(1 - OFF[s] + OFF[s - 1]), in1=tb_[:, :],
                                            op0=ALU.mult, op1=ALU.add))
            link(v.tensor_scalar(tb_[:, :], tb_[:, :], float(E - 1), None, ALU.min))
            link(v.memset(tabt[:, :, :], 0))
            for side, src in enumerate((ta, tb_)):
                link(v.tensor_scalar(t_off[:, :, side], src[:, :], float(EW), None, ALU.mult))
                link(v.tensor_copy(tabt[:, :, T_EXP + side], src[:, :]))
            link(v.tensor_copy(tabt[:, :, T_OFF:T_OFF + 2], t_off[:, :, :]))
            v.tensor_copy(tabt[:, :, T_ROW], trow[:, :]).then_inc(tab_ready, 1)

            def low(j, q):
                dve.wait_ge(xh_done, j + 1)
                v.tensor_tensor(xl[q][:, :], psA[:, 512 * q:512 * q + T], xh[q][:, :], ALU.subtract).then_inc(xl_done, 1)

            def split(j, side):
                if not isinstance(j, int) or j >= 1:
                    dve.wait_ge(y_ready, 2 * j + side - 1)
                if side == 0:
                    dve.wait_ge(g_done, 2 * j + 1)
                    v.tensor_copy(gh[0][:, :], g[0][:, :]).then_inc(hi0_done, 1)
                dve.wait_ge((hi0_done, hi1_done)[side], j + 1)
                v.tensor_tensor(gl[side][:, :], g[side][:, :], gh[side][:, :], ALU.subtract).then_inc(lo_done, 1)

            def combine(j, side, r):
                dve.wait_ge(y_ready, 2 * j + side + 1)
                for b in range(TB):
                    bank = ybank[side][:, 2 * b * D:2 * (b + 1) * D]
                    if side == 0:
                        last = v.tensor_scalar(ya[r][:, b, :], bank, rt[r][:, b, W_LO:W_LO + 1], None, ALU.mult)
                    else:
                        if b == 0:
                            dve.wait_ge(ya_done, 2 * j + 3)
                        last = v.scalar_tensor_tensor(out=ya[r][:, b, :], in0=bank, scalar=rt[r][:, b, W_HI:W_HI + 1], in1=ya[r][:, b, :],
                                                      op0=ALU.mult, op1=ALU.add)
                last.then_inc(ya_done, 1)

            dve.sem_inc(ya_done, 2)
            low(0, 0)
            low(1, 1)
            split(0, 0)
            split(0, 1)

            def dstep(j, r):
                more = not isinstance(j, int)
                if more or j + 1 < NT:
                    split(j + 1, 0)
                if more or j + 2 < NT:
                    low(j + 2, r % 2)
                combine(j, 0, r)
                if more or j + 1 < NT:
                    split(j + 1, 1)
                combine(j, 1, r)
            with dve.Fori(0, NT // 4 - 1, 1) as t:
                for r in range(4):
                    dstep(4 * t + r, r)
            for r in range(4):
                dstep(NT - 4 + r, r)

            dve.sem_inc(o_ready, 2)
            with dve.Fori(0, NIMG // 2, 1) as t:
                for q in range(2):
                    dve.wait_ge(yT_ready, 2 * t + q + 1)
                    dve.wait_ge(yx_in[q], 32 * (t + 1))
                    dve.wait_ge(o_out[q], 16 + 16 * t)
                    v.tensor_tensor(oe[q][:, :], xe[q][:, :], (psA if q == 0 else psV)[:, :], ALU.add).then_inc(o_ready, 1)


_INS = ['x', 'L0_conv_w1', 'L0_conv_b1', 'L0_conv_w2', 'L0_conv_b2', 'L0_conv_bias', 'L0_ffn_Wg', 'L0_ffn_bg',
        'L0_ffn_W1', 'L0_ffn_b1', 'L0_ffn_W2', 'L0_ffn_b2']
_OUTS = [((32, 128, 32, 32), 'float32')]


def kernel(**inputs):
    import numpy as _np
    import concourse.bacc as _bacc
    from concourse import mybir as _mybir
    from concourse.bass_utils import run_bass_kernel_spmd as _run

    nc = _bacc.Bacc("TRN2", target_bir_lowering=False, num_devices=1)
    arrays, args = {}, []
    for name in _INS:
        a = _np.ascontiguousarray(inputs[name])
        arrays[f"in_{name}_dram"] = a
        args.append(nc.dram_tensor(f"in_{name}_dram", a.shape, _mybir.dt.from_np(a.dtype), kind="ExternalInput").ap())
    for i, (shape, dtype) in enumerate(_OUTS):
        dt = _mybir.dt.from_np(_np.dtype(dtype))
        args.append(nc.dram_tensor(f"out_{i}_dram", shape, dt, kind="ExternalOutput").ap())
    conv_moe_block(nc, *args)
    r = _run(nc, [arrays], core_ids=[0])
    got = tuple(r.results[0][f"out_{i}_dram"] for i in range(len(_OUTS)))
    return got[0]
```

```python
from contextlib import ExitStack

import concourse.bass as bass
from concourse import mybir

ALU = mybir.AluOpType
ACT = mybir.ActivationFunctionType
AX_X = mybir.AxisListType.X
F32 = mybir.dt.float32
F16 = mybir.dt.float16
BF16 = mybir.dt.bfloat16
I32 = mybir.dt.int32
U32 = mybir.dt.uint32

P = 128
TAPS = 9
LN_C_EPS = 1e-6
LN_T_EPS = 1e-5
LEAST = -3e38
MASKED = -1e30
EXP_LN_TABLES = 6
WSCALE = 64.0


class Chain:

    def __init__(self, eng, sem, per_round):
        self.eng, self.sem, self.per_round, self.base, self.n = eng, sem, per_round, 0, 0

    def begin(self, n):
        self.base, self.n = n * self.per_round, 0

    def mark(self, ins):
        self.n += 1
        ins.then_inc(self.sem, 1)

    def wait(self):
        self.eng.wait_ge(self.sem, self.base + self.n)

    def link(self, ins):
        self.mark(ins)
        self.wait()

    def end(self):
        assert self.n == self.per_round, (self.n, self.per_round)


def conv_moe_block(nc, x, conv_w1, conv_b1, conv_w2, conv_b2, conv_bias, Wg, bg, W1, b1, W2, b2, out):
    NIMG, C, HH, WW = x.shape
    PIX = HH * WW
    NBLK = PIX // P
    NTOK = NIMG * PIX
    E, D, H = W1.shape
    HS = H // P
    HALF = 512
    PW, PH = WW + 2, HH + 2
    assert C == P and D == P and NBLK * P == PIX
    NU, NB2 = NIMG // 2, 2 * NBLK
    assert NIMG % 8 == 0
    CENTER = TAPS // 2
    PE_TAPS = (CENTER, 1, 3, 5)
    N_PE = len(PE_TAPS)
    G = E + 1
    DVE_TAPS = [k for k in range(TAPS) if k not in PE_TAPS]

    NPAIR = E * (E - 1) // 2
    UP_A = 2
    NUP = UP_A * (2 * E - UP_A - 1) // 2
    NREG = max(NUP, NPAIR - NUP)
    T = 2 * P
    TB = T // P
    CAP = NTOK + 2 * T
    OFF = [a * (2 * E - a - 1) // 2 for a in range(E - 1)]
    NT = NTOK // T + NPAIR
    NT_COLS = -(-NT // P)
    RW = D + 5
    W_LO, W_HI, ID, NMR, RSTD = range(D, D + 5)
    TW, T_ROW, T_EXP, T_OFF = 8, 0, 1, 4
    O_1H, O_1L, O_2, O_B2 = 0, H, 2 * H, 4 * H
    EW = 4 * H + D
    RING = 6
    assert NT % RING == 0 and RING % 6 == 0

    rows_dram = nc.dram_tensor("rows_by_pair", [NREG * CAP + T, RW], F32).ap()
    y_dram = nc.dram_tensor("token_out", [NTOK, D], F32).ap()
    tab_dram = nc.dram_tensor("tile_table", [NT_COLS * P, TW], I32).ap()

    x_v = x.rearrange("n c h w -> n c (h w)")
    out_v = out.rearrange("n c h w -> n c (h w)")
    row = lambda v, n: v.rearrange("(a n) -> a n", a=1)

    with ExitStack() as ctx:
        def sb(name, shape, dt=F32, held=ctx):
            return held.enter_context(nc.sbuf_tensor(name, shape, dt))

        def psum(name, cols):
            return ctx.enter_context(nc.psum_tensor(name, [P, cols], F32))

        def sem(name):
            return ctx.enter_context(nc.semaphore(name))

        ones = sb("ones", [P, P])
        mean_w = sb("mean_w", [P, P])
        centre_w = sb("centre_w", [P, P])
        ident = sb("ident", [P, P])
        tri = sb("tri", [P, P])
        tri_b = sb("tri_b", [P, P], BF16)
        ones_b = sb("ones_b", [P, P], BF16)
        eps_c = sb("eps_c", [P, 1])
        eps_t = sb("eps_t", [P, 1])
        desc = sb("desc", [P, E])
        pair_base = sb("pair_base", [P, NPAIR])
        tile_no = sb("tile_no", [P, NT_COLS])
        pad_rows = sb("pad_rows", [P, TB, RW])
        bias_sel = sb("bias_sel", [P, P], F16)

        stage = sb("stage", [P, E * H])
        wall = sb("wall", [P, E * EW], F16)
        wall_e = wall[:, :].rearrange("p (e w) -> p e w", w=EW)
        w2_e = wall_e[:, :, O_2:O_B2].rearrange("p e (s t d) -> p e s t d", s=HS, t=2)
        stage_1 = stage[:, :].rearrange("p (e h) -> p e h", e=E)
        stage_2 = stage[:, :].rearrange("p (e s d) -> p e s d", e=E, s=HS)
        b1col = sb("b1col", [P, E * HS])
        b1row = sb("b1row", [E * HS, P])
        b2st = sb("b2st", [P, E * D])
        b2_e = wall_e[:, :, O_B2:EW]
        b2low = sb("b2low", [P, E * D], F16)
        cw = sb("cw", [P, 2, TAPS * P])
        cwT = sb("cwT", [P, 2, TAPS, P])
        cb = sb("cb", [P, 2, TAPS])
        conv_b = sb("conv_b", [P, 1])
        wg = sb("wg", [P, E])
        wgc = sb("wgc", [P, G])
        bgrow = sb("bgrow", [1, E])
        bgb = sb("bgb", [P, E])

        psA = psum("psA", 1024)
        psV = psum("psV", 1024)
        psT = psum("psT", 1024)
        psG = psum("psG", 512)
        psR = psum("psR", 512)
        R_CNT, R_TAP = NB2 * NPAIR, (NB2 + 1) * NPAIR
        assert R_TAP + 4 * TAPS <= 512 and NB2 * G <= 512
        psVar, psConv = psV[:, 0:HALF], psV[:, HALF:2 * HALF]

        s_load = sem("weights_loaded")
        s_stage = sem("stage_loaded")
        s_const = sem("constants_made")
        s_b2 = sem("b2_loaded")
        s_high, s_low = sem("weights_high"), sem("weights_low")
        s_setup_pe = sem("setup_products")
        s_setup_act = sem("setup_act")
        s_setup_dve = sem("setup_dve")
        x_in = [sem(f"x_in{j}") for j in range(4)]
        xc_ready, sq_ready, var_ready, ln_ready, sd_ready = map(sem, ("xc_ready", "sq_ready", "var_ready", "ln_ready", "sd_ready"))
        l_ready, sum_ready = sem("l_ready"), sem("sum_ready")
        tap_ready, z_ready, ez_ready, taps_ready, diag_ready, conv_ready = map(
            sem, ("tap_ready", "z_ready", "ez_ready", "taps_ready", "diag_ready", "conv_ready"))
        cv_ready, x_used, x1_ready = map(sem, ("cv_ready", "x_used", "x1_ready"))
        tok_ready, stat_ready, ssq_ready, tln_ready, rstd_ready, kept = map(
            sem, ("tok_ready", "stat_ready", "ssq_ready", "tln_ready", "rstd_ready", "kept"))
        lg_ready, gap_ready, e2_ready, pairs_ready, rank_ready, idx_ready = map(
            sem, ("lg_ready", "gap_ready", "e2_ready", "pairs_ready", "rank_ready", "idx_ready"))
        rank_read, routed_ready = sem("rank_read"), sem("routed_ready")
        rows_out = [sem(f"rows_out{j}") for j in range(4)]
        ch_tap, ch_win, ch4, chb = map(sem, ("dve_tap_logits", "dve_window", "dve_s4", "dve_b"))
        tab_ready, tab_out, tab_in, padded = map(sem, ("tab_ready", "tab_out", "tab_in", "padded"))
        row_in = [sem(f"row_in{r}") for r in range(RING)]
        y_out = [sem(f"y_out{r}") for r in range(RING)]
        xn_done, ysum_done = sem("xn_done"), sem("ysum_done")
        xT_ready, xh_done, xl_done, h_ready, g_done, hi0_done, hi1_done, lo_done, y_ready, ya_done, yt_done = map(
            sem, ("xT_ready", "xh_done", "xl_done", "h_ready", "g_done", "hi0_done", "hi1_done", "lo_done", "y_ready",
                  "ya_done", "yt_done"))
        ye_in = [sem(f"ye_in{j}") for j in range(4)]
        yT_ready, o_ready = sem("yT_ready"), sem("o_ready")
        o_out = [sem(f"o_out{j}") for j in range(4)]

        pooled = [sb(f"pooled{p}", [P, 2, 2]) for p in range(2)]
        zt, zm, z, zd, ez = (sb(n, [P, TAPS, 2]) for n in ("zt", "zm", "z", "zd", "ez"))
        taps = [sb(f"taps{p}", [P, TAPS, 2]) for p in range(2)]
        ssq = sb("ssq", [P, NBLK])
        spent = sb("spent", [P, PIX])
        tln = sb("tln", [P, NBLK])
        negm, rstd, nmr = ([sb(f"{n}{p}", [P, NB2]) for p in range(2)] for n in ("negm", "rstd", "nmr"))
        lg, lg2, eq, sc, m1h, m2h, mh = (sb(n, [P, NB2, E]) for n in ("lg", "lg2", "eq", "sc", "m1h", "m2h", "mh"))
        m1, m2, s1, s2, gap, e2, den, wa, wb, flag, dw, fd, idf = (
            sb(n, [P, NB2]) for n in ("m1", "m2", "s1", "s2", "gap", "e2", "den", "wa", "wb", "flag", "dw", "fd", "idf"))
        pairs = sb("pairs", [P, NB2, NPAIR], BF16)
        pos = sb("pos", [P, NB2, NPAIR])
        base = sb("base", [P, NPAIR])
        idx = [sb(f"idx{p}", [P, NB2], I32) for p in range(2)]

        cnt, tiles_f, tend, zero28, ge, sel = (sb(n, [P, NPAIR]) for n in ("cnt", "tiles_f", "tend", "zero28", "ge", "sel"))
        cnt_i, tiles_i = sb("cnt_i", [P, NPAIR], I32), sb("tiles_i", [P, NPAIR], I32)
        base_i = sb("base_i", [P, NPAIR], I32)
        tp, tst, trow, ta, tb_, tt1, down_ = (sb(n, [P, NT_COLS]) for n in ("tp", "tst", "trow", "ta", "tb", "tt1", "grows_down"))
        tabt = sb("tabt", [P, NT_COLS, TW], I32)
        t_off = sb("t_off", [P, NT_COLS, 2])
        tab = sb("tab", [1, NT_COLS * P * TW], I32)

        phase_a = ExitStack()
        xb = [sb(f"xb{j}", [P, PIX], held=phase_a) for j in range(4)]
        sq = sb("sq", [P, PIX], held=phase_a)
        lnv = sb("lnv", [P, PIX], held=phase_a)
        sd = sb("sd", [P, PIX], held=phase_a)
        lp = [sb(f"lp{j}", [P, PH, PW], held=phase_a) for j in range(4)]
        x1 = [sb(f"x1_{j}", [P, PIX], held=phase_a) for j in range(4)]
        diag = [sb(f"diag{k}", [P, N_PE, P], held=phase_a) for k in range(2)]
        cv = [sb(f"cv{k}", [P, PIX], held=phase_a) for k in range(2)]
        rows = [sb(f"rows{p}", [P, NB2, RW], held=phase_a) for p in range(2)]
        phase_a.close()

        rt = [sb(f"rt{r}", [P, TB, RW]) for r in range(RING)]
        xn = [sb(f"xn{q}", [P, TB, D]) for q in range(2)]
        xh = [sb(f"xh{q}", [P, T], F16) for q in range(2)]
        xl = [sb(f"xl{q}", [P, T], F16) for q in range(2)]
        g = [sb(f"g{q}", [P, HS * T]) for q in range(2)]
        gh = [sb(f"gh{q}", [P, HS * T], F16) for q in range(2)]
        gl = [sb(f"gl{q}", [P, HS * T], F16) for q in range(2)]
        ya = [sb(f"ya{r}", [P, TB, 2 * D]) for r in range(RING)]
        yt = [sb(f"yt{r}", [P, TB, D]) for r in range(RING)]

        ye = [sb(f"ye{j}", [P, NBLK, D]) for j in range(4)]
        oe = [sb(f"oe{j}", [P, PIX]) for j in range(4)]

        inner = lambda j: lp[j][:, 1:1 + HH, 1:1 + WW]
        img = lambda t: t[:, :].rearrange("p (h w) -> p h w", w=WW)
        spread = lambda t: t[:, :].unsqueeze(2).broadcast_to([P, NB2, E])
        per_blk = lambda t, n: t[:, :].unsqueeze(1).broadcast_to([P, NB2, n])

        FIRST, LAST = 6, NU - 2

        class Step:
            def __init__(self, t, r):
                self.t, self.r, self.fixed = t, r, isinstance(t, int)
                self.first = self.fixed and t + r == 0

            def on(self, stage):
                return not self.fixed or 0 <= 2 * self.t + self.r - (stage - 1) < NU

            def count(self, stage, per, more):
                return per * 2 * self.t + (per * (self.r - (stage - 1)) + more)

            def turns(self, stage):
                return self.t + (self.r - (stage - 1)) // 2

            def next(self):
                return Step(self.t + self.r, 1 - self.r)

            def slot(self, stage):
                return (self.r - (stage - 1)) % 2

        def run_steps(eng, step):
            for s in range(FIRST):
                step(Step(s // 2, s % 2))
            with eng.Fori(FIRST // 2, LAST // 2, 1) as t:
                for r in range(2):
                    step(Step(t, r))
            for s in range(LAST, NU + 3):
                step(Step(s // 2, s % 2))

        hbank = (psV, psT)
        ybank = (psG, psR)

        def pad(eng, k):
            if k < NUP:
                first = eng.value_load(base_i[0:1, k:k + 1], min_val=k * CAP, max_val=k * CAP + NTOK)
            elif k < NPAIR:
                top = (k - NUP + 1) * CAP - 1
                first = eng.value_load(base_i[0:1, k:k + 1], min_val=top - NTOK, max_val=top) - (T - 1)
            else:
                first = NREG * CAP
            eng.dma_start(rows_dram[bass.ds(first, T), :].rearrange("(p b) f -> p b f", b=TB), pad_rows[:, :, :]).then_inc(padded, 16)

        block = ctx.enter_context(nc.Block())

        @block.sync
        def _(sp):
            for free in o_out:
                sp.sem_inc(free, 16)
            def load(n, q):
                sp.dma_start(xb[q][:, :], x_v[n] if isinstance(n, int) else x_v[bass.ds(n, 1)].rearrange("a c m -> (a c) m")).then_inc(x_in[q], 16)
            load(0, 0)
            for dst, src in (
                (cw[:, 0, :], conv_w1.rearrange("(c k) j -> c (k j)", k=TAPS)),
                (cw[:, 1, :], conv_w2.rearrange("(c k) j -> c (k j)", k=TAPS)),
                (cb[:, 0, :], conv_b1.rearrange("(c k) -> c k", k=TAPS)),
                (cb[:, 1, :], conv_b2.rearrange("(c k) -> c k", k=TAPS)),
                (conv_b[:, :], conv_bias.rearrange("(c a) -> c a", a=1)),
                (wg[:, :], Wg), (bgrow[:, :], row(bg, E)),
                (b1row[:, :], b1.rearrange("e (s p) -> (e s) p", p=P)),
            ):
                sp.dma_start(dst, src).then_inc(s_load, 16)
            for j in range(1, 4):
                load(j, j)
            sp.dma_start(stage_1, W1.rearrange("e d h -> d e h")).then_inc(s_stage, 16)
            sp.wait_ge(s_const, 1)
            b2_flat = b2.rearrange("(a e) d -> a (e d)", a=1)
            sp.dma_start(b2st[0:1, :], b2_flat).then_inc(s_b2, 16)
            sp.dma_start(b2st[32:33, :], b2_flat).then_inc(s_b2, 16)
            sp.wait_ge(s_low, 1)
            sp.dma_start(stage_2, W2.rearrange("e (s p) d -> p e s d", p=P)).then_inc(s_stage, 16)

            with sp.Fori(0, NIMG // 4 - 1, 1) as t:
                for j in range(4):
                    sp.wait_ge(x_used, 4 * t + j + 1)
                    load(4 * t + j + 4, j)

            sp.wait_ge(tab_ready, 1)
            for k in range(NPAIR // 4):
                pad(sp, k)
            sp.wait_ge(tab_ready, 2)
            sp.dma_start(tab_dram.rearrange("(c p) f -> p c f", p=P), tabt[:, :, :]).then_inc(tab_out, 16)
            for k in range(NPAIR // 4, NPAIR // 2 + 1):
                pad(sp, k)
            sp.wait_ge(tab_out, 16)
            sp.dma_start(tab[:, :], tab_dram.rearrange("(a n) f -> a (n f)", a=1)).then_inc(tab_in, 16)
            sp.wait_ge(tab_in, 16)

            for j in range(4):
                sp.wait_ge(rows_out[j], 16 * NBLK * (NIMG // 4))

            sp.wait_ge(padded, 16 * (NPAIR + 1))
            def load_rows(first, r):
                sp.dma_start(rt[r][:, :, :], rows_dram[bass.ds(first, T), :].rearrange("(p b) f -> p b f", b=TB)).then_inc(row_in[r], 16)

            for r in range(RING):
                first = sp.value_load(tab[0:1, TW * r:TW * r + 1], min_val=0, max_val=NREG * CAP)
                load_rows(first, r)
            with sp.Fori(1, NT // RING, 1) as t:
                for r in range(RING):
                    first = sp.value_load(tab[0:1, bass.ds((RING * t + r) * TW, 1)], min_val=0, max_val=NREG * CAP)
                    sp.wait_ge(y_out[r], 16 * TB * t)
                    load_rows(first, r)

            for r in range(RING):
                sp.wait_ge(y_out[r], 16 * TB * (NT // RING))
            def load_e(t, j):
                n = 4 * t + j
                sp.dma_start(ye[j][:, :, :], y_dram.rearrange("(n b p) d -> n p b d", b=NBLK, p=P)[bass.ds(n, 1)].rearrange("a p b d -> (a p) b d")).then_inc(ye_in[j], 16)
            for j in range(4):
                load_e(0, j)
            with sp.Fori(1, NIMG // 4, 1) as t:
                for j in range(4):
                    sp.wait_ge(yT_ready, 4 * t + j - 3)
                    load_e(t, j)
            for j in range(4):
                sp.wait_ge(o_out[j], 16 + 16 * (NIMG // 4))

        @block.gpsimd
        def _(pool):
            gp = nc.gpsimd
            gp.memset(b2st[:, :], 0.0).then_inc(s_const, 1)
            gp.memset(ones[:, :], 1.0)
            gp.memset(ones_b[:, :], 1.0)
            gp.memset(mean_w[:, :], 1.0 / C)
            gp.memset(eps_c[:, :], LN_C_EPS)
            gp.memset(eps_t[:, :], LN_T_EPS)
            gp.memset(bias_sel[:, :], 0.0)
            gp.memset(zero28[:, :], 0.0)
            for j in range(4):
                gp.memset(lp[j][:, :, :], 0.0)
            for p in range(2):
                gp.iota(rows[p][:, :, ID].bitcast(I32), [[P, NB2]], base=(2 * p - 4) * PIX, channel_multiplier=1)
            gp.memset(pad_rows[:, :, :], 0.0)
            gp.iota(desc[:, :], [[-1, E]], base=E, channel_multiplier=0, allow_small_or_imprecise_dtypes=True)
            gp.iota(tile_no[:, :], [[P, NT_COLS]], base=0, channel_multiplier=1, allow_small_or_imprecise_dtypes=True)
            gp.iota(pair_base[:, :], [[1, NPAIR]], base=0, channel_multiplier=0,
                    allow_small_or_imprecise_dtypes=True).then_inc(s_const, 1)
            pool.wait_ge(s_const, 2)
            gp.iota(pad_rows[:, :, ID].bitcast(I32), [[0, TB]], base=NTOK, channel_multiplier=1)
            gp.affine_select(out=ident[:, :], in_=ones[:, :], compare_op=ALU.is_equal, fill=0.0, base=0,
                             pattern=[[-1, P]], channel_multiplier=1)
            gp.affine_select(out=tri[:, :], in_=ones[:, :], compare_op=ALU.is_gt, fill=0.0, base=0,
                             pattern=[[1, P]], channel_multiplier=-1).then_inc(s_const, 1)

            routed = pool.alloc_register("routed")
            images = pool.alloc_register("images")
            tiles = pool.alloc_register("tiles")
            for reg in (routed, images, tiles):
                pool.reg_mov(reg, 0)

            with pool.Fori(0, NU // 2, 1) as t:
                for p in range(2):
                    pool.reg_alu(routed, routed, 1, ALU.add)
                    pool.reg_alu(images, images, 2, ALU.add)
                    pool.wait_ge(s_const, 3)
                    pool.wait_ge(routed_ready, routed)
                    pool.wait_ge(kept, images)
                    for b in range(NB2):
                        gp.indirect_dma_start(rows_dram, bass.IndirectOffsetOnAxis(ap=idx[p][:, b:b + 1].bitcast(U32), axis=0),
                                              rows[p][:, b, :], None).then_inc(rows_out[2 * p + b // NBLK], 16)

            with pool.Fori(0, NT // RING, 1) as t:
                for r in range(RING):
                    pool.wait_ge(ya_done, 2 * (RING * t + r) + 4)
                    gp.tensor_tensor(yt[r][:, :, :], ya[r][:, :, 0:D], ya[r][:, :, D:2 * D], ALU.add).then_inc(ysum_done, 1)
                    pool.wait_ge(ysum_done, RING * t + r + 1)
                    gp.tensor_tensor(yt[r][:, :, :], yt[r][:, :, :], rt[r][:, :, 0:D], ALU.add).then_inc(yt_done, 1)
                    pool.reg_alu(tiles, tiles, 1, ALU.add)
                    pool.wait_ge(s_const, 3)
                    pool.wait_ge(yt_done, tiles)
                    for b in range(TB):
                        gp.indirect_dma_start(y_dram, bass.IndirectOffsetOnAxis(ap=rt[r][:, b, ID:ID + 1].bitcast(U32), axis=0),
                                              yt[r][:, b, :], None, bounds_check=NTOK - 1, oob_is_err=False).then_inc(y_out[r], 16)

        @block.scalar
        def _(act):
            sc_ = nc.scalar
            for n in range(5):
                act.wait_ge(s_setup_pe, n + 1)
                k = min(4, 2 * TAPS - 4 * n)
                sc_.activation(cwT[:, :, :, :].rearrange("p a k c -> p (a k) c")[:, 4 * n:4 * n + k, :],
                               (psA if n % 2 == 0 else psV)[:, 0:k * P].rearrange("p (k c) -> p k c", c=P), ACT.Copy).then_inc(s_setup_act, 1)
            act.wait_ge(s_setup_pe, 6)
            sc_.activation(b1col[:, :], psG[:, 0:E * HS], ACT.Copy).then_inc(s_setup_act, 1)
            sc_.activation(bgb[:, :], psG[:, 64:64 + E], ACT.Copy).then_inc(s_setup_act, 1)

            def split_weights(n):
                act.wait_ge(s_stage, 16 * (n + 1))
                if n == 0:
                    sc_.activation(wall_e[:, :, O_1H:O_1L], stage_1, ACT.Copy, scale=WSCALE).then_inc(s_high, 1)
                    act.wait_ge(s_b2, 32)
                    sc_.activation(b2_e, b2st[:, :].rearrange("p (e d) -> p e d", e=E), ACT.Copy, scale=WSCALE).then_inc(s_high, 1)
                else:
                    for e in range(E):
                        last = sc_.activation(w2_e[:, e, :, 0, :], stage_2[:, e, :, :], ACT.Copy, scale=WSCALE)
                    last.then_inc(s_high, 1)

            act.wait_ge(s_const, 3)
            sc_.add_instruction(mybir.InstLoadActFuncSet(name=nc.get_next_instruction_name(), act_func_set_id=EXP_LN_TABLES, ins=[], outs=[]))

            def square(st_, k):
                act.wait_ge(xc_ready, st_.count(1, 2, k + 1))
                if not st_.fixed or st_.t + st_.r + k > 0:
                    act.wait_ge(sum_ready, st_.count(1, 2, k))
                sc_.activation(sq[:, :], psA[:, :], ACT.Square).then_inc(sq_ready, 1)

            def inv_std(st_, k, h):
                cols = slice(h * HALF, (h + 1) * HALF)
                n = st_.count(1, 4, 2 * k + h + 1)
                act.wait_ge(var_ready, n)
                sc_.activation(lnv[:, cols], psVar, ACT.Ln, bias=eps_c[:, :]).then_inc(ln_ready, 1)
                act.wait_ge(ln_ready, n)
                if not st_.fixed or st_.t + st_.r + k > 0:
                    act.wait_ge(l_ready, st_.count(1, 2, k))
                sc_.activation(sd[:, cols], lnv[:, cols], ACT.Exp, scale=-0.5).then_inc(sd_ready, 1)

            def sum_up(st_, k):
                act.wait_ge(l_ready, st_.count(1, 2, k + 1))
                sc_.activation(img(sq), inner(2 * st_.slot(1) + k), ACT.Copy, accum_out=pooled[st_.slot(1)][:, 0, k:k + 1]).then_inc(sum_ready, 1)

            def diagonals(st_, k):
                act.wait_ge(taps_ready, st_.count(2, 1, 1))
                if not st_.fixed or 2 * st_.t + st_.r > 1:
                    act.wait_ge(conv_ready, st_.count(2, 4, 2 * k - 2))
                for m, tap in enumerate(PE_TAPS):
                    last = sc_.activation(diag[k][:, m, :], ident[:, :], ACT.Copy, scale=taps[st_.slot(2)][:, tap, k:k + 1])
                last.then_inc(diag_ready, 1)

            def take(st_, k, h):
                act.wait_ge(conv_ready, st_.count(2, 4, 2 * k + h + 1))
                if not st_.fixed or 2 * st_.t + st_.r > 1:
                    act.wait_ge(x_used, st_.count(2, 2, k - 1))
                sc_.activation(cv[k][:, h * HALF:(h + 1) * HALF], psConv, ACT.Identity, bias=conv_b[:, :], scale=1.0).then_inc(cv_ready, 1)

            def token_std(st_, k):
                n = st_.count(3, 2, k + 1)
                act.wait_ge(stat_ready, n)
                for b in range(NBLK):
                    last = sc_.activation(spent[:, b * P:(b + 1) * P], psT[:, b * P:(b + 1) * P], ACT.Square, bias=negm[st_.slot(3)][:, k * NBLK + b:k * NBLK + b + 1],
                                          accum_out=ssq[:, b:b + 1])
                last.then_inc(ssq_ready, 1)
                act.wait_ge(ssq_ready, n)
                sc_.activation(tln[:, :], ssq[:, :], ACT.Ln, bias=eps_t[:, :], scale=1.0 / D).then_inc(tln_ready, 1)
                act.wait_ge(tln_ready, n)
                sc_.activation(rstd[st_.slot(3)][:, k * NBLK:(k + 1) * NBLK], tln[:, :], ACT.Exp, scale=-0.5).then_inc(rstd_ready, 1)

            def keep(st_, k):
                p = st_.slot(3)
                if not st_.fixed or st_.turns(3) > 0:
                    act.wait_ge(rows_out[2 * p + k], 16 * NBLK * st_.turns(3))
                sc_.activation(rows[p][:, k * NBLK:(k + 1) * NBLK, 0:D], psT[:, :].rearrange("p (b d) -> p b d", d=D), ACT.Copy).then_inc(kept, 1)

            def step(st_):
                if st_.first:
                    square(st_, 0)
                if st_.on(2):
                    diagonals(st_, 0)
                for k in range(2):
                    if k == 1 and st_.on(4):
                        act.wait_ge(gap_ready, st_.count(4, 1, 1))
                        sc_.activation(e2[:, :], gap[:, :], ACT.Exp).then_inc(e2_ready, 1)
                    if st_.on(1):
                        inv_std(st_, k, 0)
                    if k == 0 and st_.on(2):
                        diagonals(st_, 1)
                    if st_.on(1):
                        inv_std(st_, k, 1)
                    if st_.on(2):
                        take(st_, k, 0)
                    if st_.on(1):
                        sum_up(st_, k)
                    if st_.on(3):
                        token_std(st_, k)
                        keep(st_, k)
                    if st_.on(2):
                        take(st_, k, 1)
                    if st_.on(1):
                        if k == 0:
                            square(st_, 1)
                if st_.next().on(1):
                    square(st_.next(), 0)
                if st_.on(1):
                    act.wait_ge(z_ready, st_.count(1, 1, 1))
                    sc_.activation(ez[:, :, :], zd[:, :, :], ACT.Exp).then_inc(ez_ready, 1)
                if st_.fixed and 2 * st_.t + st_.r < 2:
                    split_weights(st_.r)

            run_steps(act, step)

            act.wait_ge(tab_ready, 1)
            for k in range(NPAIR // 2 + 1, NPAIR + 1):
                pad(act, k)

            act.wait_ge(tab_in, 16)

            def normalise(j, r, t):
                q = r % 2
                act.wait_ge(row_in[r], 16 * (t + 1))
                if not isinstance(j, int) or j >= 2:
                    act.wait_ge(xT_ready, j - 1)
                for b in range(TB):
                    last = sc_.activation(xn[q][:, b, :], rt[r][:, b, 0:D], ACT.Identity, bias=rt[r][:, b, NMR:NMR + 1], scale=rt[r][:, b, RSTD:RSTD + 1])
                last.then_inc(xn_done, 1)

            def high(j, q):
                act.wait_ge(xT_ready, j + 1)
                sc_.activation(xh[q][:, :], psA[:, 512 * q:512 * q + T], ACT.Copy).then_inc(xh_done, 1)

            def gelu(j, side):
                at = TW * j + T_EXP + side
                e = act.value_load(tab[0:1, at:at + 1] if isinstance(j, int) else tab[0:1, bass.ds(at, 1)], min_val=0, max_val=E - 1)
                act.wait_ge(h_ready, 2 * j + side + 1)
                if not isinstance(j, int) or j >= 1:
                    act.wait_ge(lo_done, 2 * j + side - 1)
                for s in range(HS):
                    last = sc_.activation(g[side][:, s * T:(s + 1) * T], hbank[side][:, s * T:(s + 1) * T], ACT.Gelu,
                                          bias=b1col[:, bass.ds(e * HS + s, 1)], scale=1.0 / WSCALE)
                last.then_inc(g_done, 1)
                if side == 1:
                    act.wait_ge(g_done, 2 * j + 2)
                    if not isinstance(j, int) or j >= 1:
                        act.wait_ge(y_ready, 2 * j)
                    sc_.activation(gh[1][:, :], g[1][:, :], ACT.Copy).then_inc(hi1_done, 1)

            normalise(0, 0, 0)
            normalise(1, 1, 0)
            high(0, 0)
            high(1, 1)
            normalise(2, 2, 0)
            gelu(0, 0)
            gelu(0, 1)

            def dstep(j, r, t):
                if not isinstance(j, int) or j + 1 < NT:
                    gelu(j + 1, 0)
                if not isinstance(j, int) or j + 2 < NT:
                    high(j + 2, r % 2)
                if not isinstance(j, int) or j + 3 < NT:
                    normalise(j + 3, (r + 3) % RING, t + (r + 3) // RING)
                if not isinstance(j, int) or j + 1 < NT:
                    gelu(j + 1, 1)
            with act.Fori(0, NT // RING - 1, 1) as t:
                for r in range(RING):
                    dstep(RING * t + r, r, t)
            for r in range(RING):
                dstep(NT - RING + r, r, NT // RING - 1)

            with act.Fori(0, NIMG // 4, 1) as t:
                for j in range(4):
                    act.wait_ge(o_ready, 4 * t + j + 3)
                    act.dma_start(out_v[bass.ds(4 * t + j, 1)].rearrange("a c m -> (a c) m"), oe[j][:, :]).then_inc(o_out[j], 16)

        @block.tensor
        def _(pe):
            te = nc.tensor
            pe.wait_ge(s_const, 3)
            pe.wait_ge(s_load, 16 * 8)
            for n in range(5):
                k = min(4, 2 * TAPS - 4 * n)
                if n >= 2:
                    pe.wait_ge(s_setup_act, n - 1)
                for m in range(k):
                    a, tap = divmod(4 * n + m, TAPS)
                    last = te.transpose((psA if n % 2 == 0 else psV)[:, m * P:(m + 1) * P], cw[:, a, tap * P:(tap + 1) * P], ident[:, :])
                last.then_inc(s_setup_pe, 1)
            te.transpose(psG[:, 0:E * HS], b1row[:, :], ident[0:E * HS, 0:E * HS])
            te.matmul(psG[:, 64:64 + E], ones[0:1, :], bgrow[:, :], start=True, stop=True)
            te.matmul(psG[:, 128:128 + E], mean_w[:, :], wg[:, :], start=True, stop=True).then_inc(s_setup_pe, 1)
            pe.wait_ge(s_setup_act, 7)
            pe.wait_ge(s_setup_dve, 2)

            def centre(st_, k, h):
                j = 2 * st_.slot(1) + k
                if h == 0:
                    pe.wait_ge(x_in[j], 16 * (st_.turns(1) + 1))
                    if not st_.fixed or st_.t + st_.r + k > 0:
                        pe.wait_ge(l_ready, st_.count(1, 2, k))
                ins = te.matmul(psA[:, h * HALF:(h + 1) * HALF], centre_w[:, :], xb[j][:, h * HALF:(h + 1) * HALF], start=True, stop=True)
                if h == 1:
                    ins.then_inc(xc_ready, 1)

            def variance(st_, k, h):
                if h == 0:
                    pe.wait_ge(sq_ready, st_.count(1, 2, k + 1))
                if not st_.fixed or st_.t + st_.r + k + h > 0:
                    pe.wait_ge(ln_ready, st_.count(1, 4, 2 * k + h))
                te.matmul(psVar, mean_w[:, :], sq[:, h * HALF:(h + 1) * HALF], start=True, stop=True).then_inc(var_ready, 1)

            def tap_logits(st_, quarter):
                if quarter == 0:
                    pe.wait_ge(sum_ready, st_.count(1, 2, 2))
                    pe.wait_ge(l_ready, st_.count(1, 2, 2))
                    if st_.on(4):
                        pe.wait_ge(rank_read, st_.count(4, 1, 1))
                for m in range(2 * TAPS * quarter // 4, 2 * TAPS * (quarter + 1) // 4):
                    a, tap = divmod(m, TAPS)
                    last = te.matmul(psR[:, R_TAP + 2 * m:R_TAP + 2 * m + 2], cwT[:, a, tap, :], pooled[st_.slot(1)][:, a, :], start=True, stop=True)
                if quarter == 3:
                    last.then_inc(tap_ready, 1)

            def turn(st_, k):
                j = 2 * st_.slot(3) + k
                pe.wait_ge(x1_ready, st_.count(3, 2, k + 1))
                if k == 0 and (not st_.fixed or st_.count(3, 1, 0) > 0):
                    pe.wait_ge(lg_ready, st_.count(3, 1, 0))
                if not st_.fixed or st_.count(3, 2, k) > 0:
                    pe.wait_ge(kept, st_.count(3, 2, k))
                for b in range(NBLK):
                    te.transpose(psT[:, b * P:(b + 1) * P], x1[j][:, b * P:(b + 1) * P], ident[:, :])
                    at = (k * NBLK + b) * G
                    last = te.matmul(psG[:, at:at + G], x1[j][:, b * P:(b + 1) * P], wgc[:, :], start=True, stop=True)
                last.then_inc(tok_ready, 1)

            def conv(st_, k, h, m):
                j = 2 * st_.slot(2) + k
                if m == 0:
                    if h == 0:
                        pe.wait_ge(diag_ready, st_.count(2, 2, k + 1))
                    if not st_.fixed or st_.count(2, 4, 2 * k + h) > 0:
                        pe.wait_ge(cv_ready, st_.count(2, 4, 2 * k + h))
                dy, dx = divmod(PE_TAPS[m], 3)
                y = dy + h * HH // 2
                ins = te.matmul(psConv.rearrange("p (h w) -> p h w", w=WW), diag[k][:, m, :], lp[j][:, y:y + HH // 2, dx:dx + WW],
                                start=(m == 0), stop=(m == N_PE - 1))
                if m == N_PE - 1:
                    ins.then_inc(conv_ready, 1)

            def ranks(st_):
                pe.wait_ge(pairs_ready, st_.count(4, 1, 1))
                if st_.on(2):
                    pe.wait_ge(z_ready, st_.count(2, 1, 1))
                elif st_.count(4, 1, 0) > 0:
                    pe.wait_ge(rank_read, st_.count(4, 1, 0))
                n = NPAIR
                te.matmul(psR[:, 0:R_CNT], tri_b[:, :], pairs[:, :, :].rearrange("p b k -> p (b k)"), start=True, stop=False, skip_group_check=True)
                for b in range(NB2):
                    left = NB2 - b
                    last = te.matmul(psR[:, (b + 1) * n:(NB2 + 1) * n].rearrange("p (b k) -> p b k", k=n), ones_b[:, :],
                                     pairs[:, b:b + 1, :].broadcast_to([P, left, n]), start=False, stop=(b == NB2 - 1), skip_group_check=True)
                last.then_inc(rank_ready, 1)

            def step(st_):
                if st_.first:
                    for h in range(2):
                        centre(st_, 0, h)
                for k in range(2):
                    if st_.on(3):
                        turn(st_, k)
                    if st_.on(1):
                        variance(st_, k, 0)
                    if st_.on(2):
                        for m in range(2):
                            conv(st_, k, 0, m)
                    if st_.on(1):
                        variance(st_, k, 1)
                    if st_.on(2):
                        for m in range(2, N_PE):
                            conv(st_, k, 0, m)
                    if k == 1 and st_.on(4):
                        ranks(st_)
                    if st_.on(2):
                        for m in range(N_PE if k == 0 else N_PE - 2):
                            conv(st_, k, 1, m)
                    if k == 0 and st_.on(1):
                        for h in range(2):
                            centre(st_, 1, h)
                for quarter in range(4):
                    if quarter < 2:
                        if st_.on(2):
                            conv(st_, 1, 1, N_PE - 2 + quarter)
                    elif st_.next().on(1):
                        centre(st_.next(), 0, quarter - 2)
                    if st_.on(1):
                        tap_logits(st_, quarter)

            run_steps(pe, step)

            pe.wait_ge(tab_in, 16)
            pe.wait_ge(s_low, 3)
            pe.wait_ge(idx_ready, NU)

            off = [[pe.alloc_register(f"off{q}{side}") for side in range(2)] for q in range(3)]

            def experts(j, q):
                at = TW * j + T_OFF
                pe.load(off[q], tab[0:1, at:at + 2] if isinstance(j, int) else tab[0:1, bass.ds(at, 2)])

            def weights(q, side):
                return pe.snap(off[q][side], min_val=0, max_val=(E - 1) * EW)

            def turn_rows(j, r):
                pe.wait_ge(xn_done, j + 1)
                if not isinstance(j, int) or j >= 2:
                    pe.wait_ge(xl_done, j - 1)
                    pe.wait_ge(xh_done, j - 1)
                for b in range(TB):
                    last = te.transpose(psA[:, 512 * (r % 2) + b * P:512 * (r % 2) + (b + 1) * P], xn[r % 2][:, b, :], ident[:, :])
                last.then_inc(xT_ready, 1)

            def up(j, side, q, o):
                w = weights(o, side)
                pe.wait_ge(xh_done, j + 1)
                pe.wait_ge(xl_done, j + 1)
                if not isinstance(j, int) or j >= 1:
                    pe.wait_ge(g_done, 2 * j + side - 1)
                for s in range(HS):
                    out_ = hbank[side][:, s * T:(s + 1) * T]
                    high = wall[:, bass.ds(w + (O_1H + s * P), P)]
                    te.matmul(out_, high, xh[q][:, :], start=True, stop=False)
                    te.matmul(out_, high, xl[q][:, :], start=False, stop=False)
                    last = te.matmul(out_, wall[:, bass.ds(w + (O_1L + s * P), P)], xh[q][:, :], start=False, stop=True)
                last.then_inc(h_ready, 1)

            def down(j, side, o):
                w = weights(o, side)
                pe.wait_ge(lo_done, 2 * j + side + 1)
                pe.wait_ge((hi0_done, hi1_done)[side], j + 1)
                pe.wait_ge(ya_done, 2 * j + side + 1)
                bank = ybank[side]
                for s in range(HS):
                    both = wall[:, bass.ds(w + (O_2 + 2 * s * D), 2 * D)]
                    high = wall[:, bass.ds(w + (O_2 + 2 * s * D), D)]
                    for b in range(TB):
                        lhs = slice(s * T + b * P, s * T + (b + 1) * P)
                        te.matmul(bank[:, 2 * b * D:2 * (b + 1) * D], gh[side][:, lhs], both, start=(s == 0 and b == 0), stop=False, skip_group_check=True)
                        te.matmul(bank[:, 2 * b * D:(2 * b + 1) * D], gl[side][:, lhs], high, start=False, stop=False, skip_group_check=True)
                bias = wall[:, bass.ds(w + O_B2, D)]
                for b in range(TB):
                    last = te.matmul(bank[:, 2 * b * D:(2 * b + 1) * D], bias_sel[:, :], bias, start=False, stop=(b == TB - 1), skip_group_check=True)
                last.then_inc(y_ready, 1)

            experts(0, 0)
            experts(1, 1)
            turn_rows(0, 0)
            turn_rows(1, 1)
            up(0, 0, 0, 0)
            up(0, 1, 0, 0)

            def dstep(j, r):
                more, q = not isinstance(j, int), r % 2
                if more or j + 1 < NT:
                    up(j + 1, 0, 1 - q, (r + 1) % 3)
                if more or j + 2 < NT:
                    turn_rows(j + 2, r)
                down(j, 0, r % 3)
                if more or j + 2 < NT:
                    experts(j + 2, (r + 2) % 3)
                if more or j + 1 < NT:
                    up(j + 1, 1, 1 - q, (r + 1) % 3)
                down(j, 1, r % 3)
            with pe.Fori(0, NT // RING - 1, 1) as t:
                for r in range(RING):
                    dstep(RING * t + r, r)
            for r in range(RING):
                dstep(NT - RING + r, r)

            with pe.Fori(0, NIMG // 4, 1) as t:
                for j in range(4):
                    pe.wait_ge(ye_in[j], 16 * (t + 1))
                    pe.wait_ge(o_ready, 4 * t + j + 1)
                    for b in range(NBLK):
                        last = te.transpose((psA if j % 2 == 0 else psV)[:, b * P:(b + 1) * P], ye[j][:, b, :], ident[:, :])
                    last.then_inc(yT_ready, 1)

        @block.vector
        def _(dve):
            v = nc.vector
            dve.wait_ge(s_const, 3)
            v.memset(bias_sel[0:1, :], 1.0)
            v.memset(bias_sel[32:33, :], 1.0)
            v.tensor_copy(tri_b[:, :], tri[:, :])
            v.tensor_tensor(centre_w[:, :], ident[:, :], mean_w[:, :], ALU.subtract)
            v.tensor_scalar(pair_base[:, 0:NUP], pair_base[:, 0:NUP], float(CAP), None, ALU.mult)
            v.tensor_scalar(pair_base[:, NUP:NPAIR], pair_base[:, NUP:NPAIR], float(CAP), float(CAP * (1 - NUP) - 1), ALU.mult, ALU.add).then_inc(s_setup_dve, 1)
            dve.wait_ge(s_setup_dve, 1)
            v.tensor_copy(base[:, :], pair_base[:, :])
            dve.wait_ge(s_setup_act, 7)
            v.memset(wgc[:, E:G], 1.0 / D)
            v.tensor_tensor(wgc[:, 0:E], wg[:, :], psG[:, 128:128 + E], ALU.subtract).then_inc(s_setup_dve, 1)

            def split_weights(n):
                if n == 0:
                    dve.wait_ge(s_high, 1)
                    v.scalar_tensor_tensor(out=wall_e[:, :, O_1L:O_2], in0=stage_1, scalar=WSCALE, in1=wall_e[:, :, O_1H:O_1L], op0=ALU.mult, op1=ALU.subtract).then_inc(s_low, 1)
                    dve.wait_ge(s_high, 2)
                    v.scalar_tensor_tensor(out=b2low[:, :].rearrange("p (e d) -> p e d", e=E), in0=b2st[:, :].rearrange("p (e d) -> p e d", e=E), scalar=WSCALE, in1=b2_e, op0=ALU.mult, op1=ALU.subtract).then_inc(s_setup_dve, 1)
                    dve.wait_ge(s_setup_dve, 3)
                    v.tensor_copy(b2_e[32:33], b2low[32:33, :].rearrange("p (e d) -> p e d", e=E)).then_inc(s_low, 1)
                else:
                    dve.wait_ge(s_high, 3)
                    for e in range(E):
                        last = v.scalar_tensor_tensor(out=w2_e[:, e, :, 1, :], in0=stage_2[:, e, :, :], scalar=WSCALE, in1=w2_e[:, e, :, 0, :], op0=ALU.mult, op1=ALU.subtract)
                    last.then_inc(s_low, 1)

            sd_count = dve.alloc_register("sd_count")
            c_tap = Chain(dve, ch_tap, 6)
            c_win = Chain(dve, ch_win, len(DVE_TAPS) - 1)
            c4 = Chain(dve, ch4, 26)

            def norm(st_, k):
                j = 2 * st_.slot(1) + k
                dve.reg_mov(sd_count, st_.count(1, 4, 2 * k + 2))
                dve.wait_ge(s_const, 3)
                dve.wait_ge(sd_ready, sd_count)
                v.tensor_tensor_reduce(inner(j), img(psA), img(sd), 1.0, LEAST, ALU.mult, ALU.max, pooled[st_.slot(1)][:, 1, k:k + 1]).then_inc(l_ready, 1)

            def tap_softmax(st_):
                link = c_tap.link
                c_tap.begin(st_.count(1, 1, 0))
                prod = lambda a: psR[:, R_TAP + 2 * a * TAPS:R_TAP + 2 * (a + 1) * TAPS].rearrange("p (t k) -> p t k", k=2)
                both = lambda t: t.unsqueeze(2).broadcast_to([P, TAPS, 2])
                w = taps[st_.slot(1)]
                dve.wait_ge(tap_ready, st_.count(1, 1, 1))
                v.scalar_tensor_tensor(out=zt[:, :, :], in0=prod(0), scalar=1.0 / PIX, in1=both(cb[:, 0, :]), op0=ALU.mult, op1=ALU.add)
                link(v.tensor_tensor(zm[:, :, :], prod(1), both(cb[:, 1, :]), ALU.add))
                link(v.tensor_tensor(z[:, :, :], zm[:, :, :], zt[:, :, :], ALU.subtract))
                link(v.tensor_reduce(zt[:, :, :], z[:, :, :].unsqueeze(3), AX_X, ALU.max))
                v.tensor_tensor(zd[:, :, :], z[:, :, :], zt[:, :, :], ALU.subtract).then_inc(z_ready, 1)
                dve.wait_ge(ez_ready, st_.count(1, 1, 1))
                link(v.tensor_reduce(zm[:, :, :], ez[:, :, :].unsqueeze(3), AX_X, ALU.add))
                link(v.reciprocal(zt[:, :, :], zm[:, :, :]))
                link(v.tensor_tensor(w[:, :, :], ez[:, :, :], zt[:, :, :], ALU.mult))
                v.tensor_scalar(w[:, CENTER, :], w[:, CENTER, :], 1.0, None, ALU.add).then_inc(taps_ready, 1)
                c_tap.end()

            def add_image(st_, k):
                j = 2 * st_.slot(2) + k
                dve.wait_ge(cv_ready, st_.count(2, 4, 2 * k + 2))
                v.tensor_tensor(x1[j][:, :], cv[k][:, :], xb[j][:, :], ALU.add).then_inc(x_used, 1)

            def window(st_, stage, k, part):
                j, n = 2 * st_.slot(stage) + k, st_.count(stage, 2, k)
                if part == 0:
                    c_win.begin(n)
                    dve.wait_ge(x_used, n + 1)
                for m in (range(2 + k), range(2 + k, len(DVE_TAPS)))[part]:
                    dy, dx = divmod(DVE_TAPS[m], 3)
                    ins = v.scalar_tensor_tensor(out=img(x1[j]), in0=lp[j][:, dy:dy + HH, dx:dx + WW],
                                                 scalar=taps[st_.slot(stage)][:, DVE_TAPS[m], k:k + 1],
                                                 in1=img(x1[j]), op0=ALU.mult, op1=ALU.add)
                    if m < len(DVE_TAPS) - 1:
                        c_win.link(ins)
                    else:
                        ins.then_inc(x1_ready, 1)

            gates = psG[:, 0:NB2 * G].rearrange("p (b g) -> p b g", g=G)

            def means(st_, k):
                blks = slice(k * NBLK, (k + 1) * NBLK)
                dve.wait_ge(tok_ready, st_.count(3, 2, k + 1))
                v.tensor_scalar(negm[st_.slot(3)][:, blks], gates[:, blks, E], -1.0, None, ALU.mult).then_inc(stat_ready, 1)

            def shifts(st_, k):
                blks, p = slice(k * NBLK, (k + 1) * NBLK), st_.slot(3)
                dve.wait_ge(rstd_ready, st_.count(3, 2, k + 1))
                v.tensor_tensor(nmr[p][:, blks], negm[p][:, blks], rstd[p][:, blks], ALU.mult)
                if k == 1:
                    v.tensor_tensor(lg[:, :, :], gates[:, :, 0:E], spread(rstd[p]), ALU.mult).then_inc(lg_ready, 1)

            def choose(st_):
                link = c4.link
                c4.begin(st_.count(4, 1, 0))
                dve.wait_ge(lg_ready, st_.count(4, 1, 1))
                link(v.tensor_tensor(lg[:, :, :], lg[:, :, :], per_blk(bgb, E), ALU.add))
                for n, (src, mx, s, mask) in enumerate(((lg, m1, s1, m1h), (lg2, m2, s2, m2h))):
                    if n == 1:
                        link(v.scalar_tensor_tensor(out=lg2[:, :, :], in0=m1h[:, :, :], scalar=MASKED, in1=lg[:, :, :], op0=ALU.mult, op1=ALU.add))
                    link(v.tensor_reduce(mx[:, :], src[:, :, :], AX_X, ALU.max))
                    link(v.tensor_tensor(eq[:, :, :], src[:, :, :], spread(mx), ALU.is_equal))
                    link(v.tensor_tensor(sc[:, :, :], eq[:, :, :], per_blk(desc, E), ALU.mult))
                    link(v.tensor_reduce(s[:, :], sc[:, :, :], AX_X, ALU.max))
                    link(v.tensor_tensor(mask[:, :, :], sc[:, :, :], spread(s), ALU.is_equal))
                v.tensor_tensor(gap[:, :], m2[:, :], m1[:, :], ALU.subtract).then_inc(gap_ready, 1)
                link(v.tensor_tensor(mh[:, :, :], m1h[:, :, :], m2h[:, :, :], ALU.add))
                for a in range(E - 1):
                    n = E - 1 - a
                    last = v.scalar_tensor_tensor(out=pairs[:, :, OFF[a]:OFF[a] + n], in0=mh[:, :, a + 1:E], scalar=1.0 if a < UP_A else -1.0,
                                                  in1=mh[:, :, a:a + 1].broadcast_to([P, NB2, n]), op0=ALU.mult, op1=ALU.mult)
                last.then_inc(pairs_ready, 1)

            def weigh(st_):
                link = c4.link
                r_ = rows[st_.slot(4)]
                dve.wait_ge(e2_ready, st_.count(4, 1, 1))
                link(v.tensor_scalar(den[:, :], e2[:, :], WSCALE, WSCALE, ALU.mult, ALU.add))
                link(v.reciprocal(wa[:, :], den[:, :]))
                link(v.tensor_tensor(wb[:, :], e2[:, :], wa[:, :], ALU.mult))
                link(v.tensor_tensor(flag[:, :], s1[:, :], s2[:, :], ALU.is_gt))
                link(v.tensor_tensor(dw[:, :], wa[:, :], wb[:, :], ALU.subtract))
                link(v.tensor_tensor(fd[:, :], flag[:, :], dw[:, :], ALU.mult))
                dve.wait_ge(kept, st_.count(4, 2, 2))
                link(v.tensor_tensor(r_[:, :, W_LO], wb[:, :], fd[:, :], ALU.add))
                link(v.tensor_tensor(r_[:, :, W_HI], wa[:, :], fd[:, :], ALU.subtract))
                v.tensor_copy(r_[:, :, NMR], nmr[st_.slot(4)][:, :])
                link(v.tensor_copy(r_[:, :, RSTD], rstd[st_.slot(4)][:, :]))
                dve.wait_ge(idx_ready, st_.count(4, 1, 1))
                v.tensor_scalar(r_[:, :, ID].bitcast(I32), r_[:, :, ID].bitcast(I32), 4 * PIX, None, ALU.add).then_inc(routed_ready, 1)
                c4.end()

            def place(st_):
                link = c4.link
                dve.wait_ge(rank_ready, st_.count(4, 1, 1))
                dve.wait_ge(pairs_ready, st_.count(4, 1, 1))
                link(v.tensor_tensor(pos[:, :, :], psR[:, 0:R_CNT].rearrange("p (b k) -> p b k", k=NPAIR), per_blk(base, NPAIR), ALU.add))
                v.tensor_tensor(base[:, :], base[:, :], psR[:, R_CNT:R_CNT + NPAIR], ALU.add).then_inc(rank_read, 1)
                link(v.tensor_tensor(pos[:, :, :], pos[:, :, :], pairs[:, :, :], ALU.mult))
                link(v.tensor_reduce(idf[:, :], pos[:, :, :], AX_X, ALU.add))
                link(v.scalar_tensor_tensor(out=idf[:, :], in0=idf[:, :], scalar=-1.0, in1=idf[:, :], op0=ALU.mult, op1=ALU.max))
                if not st_.fixed or st_.turns(4) > 0:
                    for k in range(2):
                        dve.wait_ge(rows_out[2 * st_.slot(4) + k], 16 * NBLK * st_.turns(4))
                v.tensor_copy(idx[st_.slot(4)][:, :], idf[:, :]).then_inc(idx_ready, 1)

            def step(st_):
                if st_.on(3):
                    means(st_, 0)
                    window(st_, 3, 1, 0)
                if st_.on(1):
                    norm(st_, 0)
                if st_.on(3):
                    window(st_, 3, 1, 1)
                if st_.on(4):
                    choose(st_)
                if st_.on(3):
                    shifts(st_, 0)
                if st_.on(2):
                    add_image(st_, 0)
                if st_.on(3):
                    means(st_, 1)
                if st_.on(2):
                    window(st_, 2, 0, 0)
                if st_.on(1):
                    norm(st_, 1)
                if st_.on(4):
                    place(st_)
                    weigh(st_)
                if st_.on(2):
                    window(st_, 2, 0, 1)
                if st_.on(3):
                    shifts(st_, 1)
                if st_.on(1):
                    tap_softmax(st_)
                if st_.on(2):
                    add_image(st_, 1)
                if st_.fixed and 2 * st_.t + st_.r < 2:
                    split_weights(st_.r)

            run_steps(dve, step)

            cb_ = Chain(dve, chb, 0)
            link = cb_.link
            dve.wait_ge(idx_ready, NU)
            v.tensor_copy(base_i[:, :], base[:, :]).then_inc(tab_ready, 1)
            link(v.tensor_tensor(cnt[:, :], base[:, :], pair_base[:, :], ALU.subtract))
            link(v.scalar_tensor_tensor(out=cnt[:, :], in0=cnt[:, :], scalar=-1.0, in1=cnt[:, :], op0=ALU.mult, op1=ALU.max))
            link(v.tensor_scalar(cnt[:, :], cnt[:, :], float(T - 1), None, ALU.add))
            link(v.tensor_copy(cnt_i[:, :], cnt[:, :]))
            link(v.tensor_scalar(tiles_i[:, :], cnt_i[:, :], T.bit_length() - 1, None, ALU.arith_shift_right))
            link(v.tensor_copy(tiles_f[:, :], tiles_i[:, :]))
            link(v.tensor_tensor_scan(tend[:, :], tiles_f[:, :], zero28[:, :], 0.0, ALU.add, ALU.add))
            for c in range(NT_COLS):
                link(v.tensor_scalar(ge[:, :], tend[:, :], tile_no[:, c:c + 1], None, ALU.is_le))
                link(v.tensor_reduce(tp[:, c:c + 1], ge[:, :], AX_X, ALU.add))
                link(v.tensor_tensor(sel[:, :], ge[:, :], tend[:, :], ALU.mult))
                link(v.tensor_reduce(tst[:, c:c + 1], sel[:, :], AX_X, ALU.max))
            link(v.tensor_scalar(trow[:, :], tp[:, :], float(CAP), None, ALU.mult))
            link(v.tensor_tensor(tt1[:, :], tile_no[:, :], tst[:, :], ALU.subtract))
            link(v.scalar_tensor_tensor(out=trow[:, :], in0=tt1[:, :], scalar=float(T), in1=trow[:, :], op0=ALU.mult, op1=ALU.add))
            link(v.tensor_scalar(down_[:, :], tp[:, :], float(NUP), None, ALU.is_ge))
            link(v.tensor_tensor(tt1[:, :], tt1[:, :], down_[:, :], ALU.mult))
            link(v.scalar_tensor_tensor(out=trow[:, :], in0=tt1[:, :], scalar=float(-2 * T), in1=trow[:, :], op0=ALU.mult, op1=ALU.add))
            link(v.scalar_tensor_tensor(out=trow[:, :], in0=down_[:, :], scalar=float(CAP - T - NUP * CAP), in1=trow[:, :], op0=ALU.mult, op1=ALU.add))
            link(v.tensor_scalar(trow[:, :], trow[:, :], float(NREG * CAP), None, ALU.min))
            link(v.memset(ta[:, :], 0.0))
            link(v.tensor_scalar(tb_[:, :], tp[:, :], 1.0, None, ALU.add))
            for s in range(1, E - 1):
                link(v.tensor_scalar(tt1[:, :], tp[:, :], float(OFF[s]), None, ALU.is_ge))
                link(v.tensor_tensor(ta[:, :], ta[:, :], tt1[:, :], ALU.add))
                link(v.scalar_tensor_tensor(out=tb_[:, :], in0=tt1[:, :], scalar=float(1 - OFF[s] + OFF[s - 1]), in1=tb_[:, :],
                                            op0=ALU.mult, op1=ALU.add))
            link(v.tensor_scalar(tb_[:, :], tb_[:, :], float(E - 1), None, ALU.min))
            link(v.memset(tabt[:, :, :], 0))
            for side, src in enumerate((ta, tb_)):
                link(v.tensor_scalar(t_off[:, :, side], src[:, :], float(EW), None, ALU.mult))
                link(v.tensor_copy(tabt[:, :, T_EXP + side], src[:, :]))
            link(v.tensor_copy(tabt[:, :, T_OFF:T_OFF + 2], t_off[:, :, :]))
            v.tensor_copy(tabt[:, :, T_ROW], trow[:, :]).then_inc(tab_ready, 1)

            def low(j, q):
                dve.wait_ge(xh_done, j + 1)
                v.tensor_tensor(xl[q][:, :], psA[:, 512 * q:512 * q + T], xh[q][:, :], ALU.subtract).then_inc(xl_done, 1)

            def split(j, side):
                if not isinstance(j, int) or j >= 1:
                    dve.wait_ge(y_ready, 2 * j + side - 1)
                if side == 0:
                    dve.wait_ge(g_done, 2 * j + 1)
                    v.tensor_copy(gh[0][:, :], g[0][:, :]).then_inc(hi0_done, 1)
                dve.wait_ge((hi0_done, hi1_done)[side], j + 1)
                v.tensor_tensor(gl[side][:, :], g[side][:, :], gh[side][:, :], ALU.subtract).then_inc(lo_done, 1)

            def combine(j, side, r):
                dve.wait_ge(y_ready, 2 * j + side + 1)
                for b in range(TB):
                    bank = ybank[side][:, 2 * b * D:2 * (b + 1) * D]
                    if side == 0:
                        last = v.tensor_scalar(ya[r][:, b, :], bank, rt[r][:, b, W_LO:W_LO + 1], None, ALU.mult)
                    else:
                        if b == 0:
                            dve.wait_ge(ya_done, 2 * j + 3)
                        last = v.scalar_tensor_tensor(out=ya[r][:, b, :], in0=bank, scalar=rt[r][:, b, W_HI:W_HI + 1], in1=ya[r][:, b, :],
                                                      op0=ALU.mult, op1=ALU.add)
                last.then_inc(ya_done, 1)

            dve.sem_inc(ya_done, 2)
            low(0, 0)
            low(1, 1)
            split(0, 0)
            split(0, 1)

            def dstep(j, r):
                more = not isinstance(j, int)
                if more or j + 1 < NT:
                    split(j + 1, 0)
                if more or j + 2 < NT:
                    low(j + 2, r % 2)
                combine(j, 0, r)
                if more or j + 1 < NT:
                    split(j + 1, 1)
                combine(j, 1, r)
            with dve.Fori(0, NT // RING - 1, 1) as t:
                for r in range(RING):
                    dstep(RING * t + r, r)
            for r in range(RING):
                dstep(NT - RING + r, r)

            dve.sem_inc(o_ready, 2)
            with dve.Fori(0, NIMG // 4, 1) as t:
                for j in range(4):
                    dve.wait_ge(yT_ready, 4 * t + j + 1)
                    dve.wait_ge(o_out[j], 16 + 16 * t)
                    v.tensor_copy(oe[j][:, :], (psA if j % 2 == 0 else psV)[:, :]).then_inc(o_ready, 1)


_INS = ['x', 'L0_conv_w1', 'L0_conv_b1', 'L0_conv_w2', 'L0_conv_b2', 'L0_conv_bias', 'L0_ffn_Wg', 'L0_ffn_bg',
        'L0_ffn_W1', 'L0_ffn_b1', 'L0_ffn_W2', 'L0_ffn_b2']
_OUTS = [((32, 128, 32, 32), 'float32')]


def kernel(**inputs):
    import numpy as _np
    import concourse.bacc as _bacc
    from concourse import mybir as _mybir
    from concourse.bass_utils import run_bass_kernel_spmd as _run

    nc = _bacc.Bacc("TRN2", target_bir_lowering=False, num_devices=1)
    arrays, args = {}, []
    for name in _INS:
        a = _np.ascontiguousarray(inputs[name])
        arrays[f"in_{name}_dram"] = a
        args.append(nc.dram_tensor(f"in_{name}_dram", a.shape, _mybir.dt.from_np(a.dtype), kind="ExternalInput").ap())
    for i, (shape, dtype) in enumerate(_OUTS):
        dt = _mybir.dt.from_np(_np.dtype(dtype))
        args.append(nc.dram_tensor(f"out_{i}_dram", shape, dt, kind="ExternalOutput").ap())
    conv_moe_block(nc, *args)
    r = _run(nc, [arrays], core_ids=[0])
    got = tuple(r.results[0][f"out_{i}_dram"] for i in range(len(_OUTS)))
    return got[0]
```
